# Optimizing a Trainium2 kernel written in Bass

```python
import numpy as np
import jax
import jax.numpy as jnp

def _softmax(x, axis=-1):
    return jax.nn.softmax(x, axis=axis)

def _gelu(x):
    return jax.nn.gelu(x, approximate=True)

def _silu(x):
    return jax.nn.silu(x)

def _sigmoid(x):
    return jax.nn.sigmoid(x)

def _layernorm(x, axis=-1, eps=1e-05):
    m = jnp.mean(x, axis=axis, keepdims=True)
    v = jnp.var(x, axis=axis, keepdims=True)
    return (x - m) / jnp.sqrt(v + eps)

def _scatter_add(tgt, idx, src, axis=0):
    return tgt.at[idx].add(src)

def _segment_sum(src, seg, n):
    return jax.ops.segment_sum(src, seg, n)
kernel_name = 'mk_adj_preln_d1_adj_r2_66b612'

def setup_inputs(seed: int=0):
    np.random.seed(seed)
    _w = jnp.asarray

    def _rec_inputs():
        import jax
        import jax.numpy as jnp
        _gk = jax.random.key(seed)
        x = -0.0005207 + 1.001 * jax.random.normal(jax.random.fold_in(_gk, 1), (8, 1024, 128), jnp.float32)
        _w = (1.0 + jnp.arange(1024, dtype=jnp.float32)) ** (-0.5)
        _w = _w / _w.mean()
        _pij = jnp.clip(0.015625 * _w[:, None] * _w[None, :], 0.0, 1.0)
        _a = jax.random.uniform(jax.random.fold_in(_gk, 2), (8, 1024, 1024)) < _pij
        _a = jnp.logical_or(_a, jnp.swapaxes(_a, -1, -2))
        _af = _a.astype(jnp.float32)
        adj = _af
        _nm = jnp.ones((8, 1024), dtype=bool)
        nodemask = jnp.where(_nm, 1.0, 0.0).astype(jnp.int32)
        return (x, adj, nodemask)
    x, adj, nodemask = _rec_inputs()

    def _L0_gnn_setup():
        import jax, jax.numpy as jnp
        import numpy as np
        T_DIL = 10
        K_DIL = 2
        BN_EPS = 1e-05
        NORM_EPS = 1e-12

        def _dilate_pattern(adj_bool, mask_b):
            N = adj_bool.shape[0]

            def step(carry, n):
                row = jnp.take(carry, n, axis=0)
                nbi = row.astype(jnp.int32)
                num = jnp.sum(nbi)
                sf = jnp.where(num > T_DIL, (num + K_DIL - 1) // K_DIL, 1)
                rank = jnp.cumsum(nbi)
                rm = row & (rank % sf == 0)
                valid = (mask_b[n] != 0) & (num > 1)
                rm = jnp.where(valid, rm, False)
                keep = ~rm
                carry = carry.at[n].set(row & keep)
                carry = carry.at[:, n].set(carry[:, n] & keep)
                return (carry, None)
            out, _ = jax.lax.scan(step, adj_bool, jnp.arange(N))
            return out

        def _dilate(adj, mask):
            keep = jax.vmap(_dilate_pattern)(adj > 0, mask)
            return adj * keep.astype(adj.dtype)

        def _sage(x, adj, Wr, Wx, b, mf):
            deg = jnp.clip(jnp.sum(adj, axis=-1, keepdims=True), 1.0, None)
            agg = jnp.einsum('bij,bjd->bid', adj, x) / deg
            out = agg @ Wr + x @ Wx + b
            nrm = jnp.maximum(jnp.linalg.norm(out, axis=-1, keepdims=True), NORM_EPS)
            return out / nrm * mf[..., None]

        def _bn(x, g, b):
            m = jnp.mean(x, axis=(0, 1))
            v = jnp.var(x, axis=(0, 1))
            return (x - m) * jax.lax.rsqrt(v + BN_EPS) * g + b

        def _forward(x, adj, mask, Wr1, Wx1, b1, g1, be1, Wr2, Wx2, b2, g2, be2, Wr3, Wx3, b3, g3, be3, Wl, bl):
            mf = mask.astype(x.dtype)
            adj_d = _dilate(adj, mask)
            h1 = _bn(jax.nn.relu(_sage(x, adj_d, Wr1, Wx1, b1, mf)), g1, be1)
            h2 = _bn(jax.nn.relu(_sage(h1, adj_d, Wr2, Wx2, b2, mf)), g2, be2)
            h3 = _bn(jax.nn.relu(_sage(h2, adj_d, Wr3, Wx3, b3, mf)), g3, be3)
            xc = jnp.concatenate([h1, h2, h3], axis=-1) * mf[..., None]
            return (xc @ Wl + bl) * mf[..., None]
        B, N, D, H, E = (8, 1024, 128, 128, 128)
        key = jax.random.key(seed)
        ks = jax.random.split(key, 24)
        x = jax.random.normal(ks[0], (B, N, D), dtype=jnp.float32)
        a = jax.random.bernoulli(ks[1], 0.01, (B, N, N))
        a = a | jnp.swapaxes(a, 1, 2)
        a = a & ~jnp.eye(N, dtype=bool)[None]
        adj = a.astype(jnp.float32)
        mask = jnp.ones((B, N), dtype=jnp.int32)
        s = 0.05
        p = {}
        dims = [(D, H), (H, H), (H, E)]
        for i, (di, do) in enumerate(dims, 1):
            p[f'Wr{i}'] = s * jax.random.normal(ks[2 * i], (di, do), dtype=jnp.float32)
            p[f'Wx{i}'] = s * jax.random.normal(ks[2 * i + 1], (di, do), dtype=jnp.float32)
            p[f'b{i}'] = jnp.zeros((do,), dtype=jnp.float32)
            p[f'g{i}'] = jnp.ones((do,), dtype=jnp.float32)
            p[f'be{i}'] = jnp.zeros((do,), dtype=jnp.float32)
        p['Wl'] = s * jax.random.normal(ks[10], (2 * H + E, E), dtype=jnp.float32)
        p['bl'] = jnp.zeros((E,), dtype=jnp.float32)
        return {'x': x, 'adj': adj, 'mask': mask, **p}
    _L0_gnn_all = _L0_gnn_setup()
    _L0_gnn_in = {k: v for k, v in _L0_gnn_all.items() if k in ('Wr1', 'Wx1', 'b1', 'g1', 'be1', 'Wr2', 'Wx2', 'b2', 'g2', 'be2', 'Wr3', 'Wx3', 'b3', 'g3', 'be3', 'Wl', 'bl')}
    del _L0_gnn_all
    return {'x': x, 'adj': adj, 'nodemask': nodemask, 'L0_gnn_Wr1': _L0_gnn_in['Wr1'], 'L0_gnn_Wx1': _L0_gnn_in['Wx1'], 'L0_gnn_b1': _L0_gnn_in['b1'], 'L0_gnn_g1': _L0_gnn_in['g1'], 'L0_gnn_be1': _L0_gnn_in['be1'], 'L0_gnn_Wr2': _L0_gnn_in['Wr2'], 'L0_gnn_Wx2': _L0_gnn_in['Wx2'], 'L0_gnn_b2': _L0_gnn_in['b2'], 'L0_gnn_g2': _L0_gnn_in['g2'], 'L0_gnn_be2': _L0_gnn_in['be2'], 'L0_gnn_Wr3': _L0_gnn_in['Wr3'], 'L0_gnn_Wx3': _L0_gnn_in['Wx3'], 'L0_gnn_b3': _L0_gnn_in['b3'], 'L0_gnn_g3': _L0_gnn_in['g3'], 'L0_gnn_be3': _L0_gnn_in['be3'], 'L0_gnn_Wl': _L0_gnn_in['Wl'], 'L0_gnn_bl': _L0_gnn_in['bl']}

def reference(x, adj, nodemask, L0_gnn_Wr1, L0_gnn_Wx1, L0_gnn_b1, L0_gnn_g1, L0_gnn_be1, L0_gnn_Wr2, L0_gnn_Wx2, L0_gnn_b2, L0_gnn_g2, L0_gnn_be2, L0_gnn_Wr3, L0_gnn_Wx3, L0_gnn_b3, L0_gnn_g3, L0_gnn_be3, L0_gnn_Wl, L0_gnn_bl):
    import jax
    import jax.numpy as jnp

    def _L0_gnn_ref(x, adj, mask, Wr1, Wx1, b1, g1, be1, Wr2, Wx2, b2, g2, be2, Wr3, Wx3, b3, g3, be3, Wl, bl):
        import jax, jax.numpy as jnp
        import numpy as np
        T_DIL = 10
        K_DIL = 2
        BN_EPS = 1e-05
        NORM_EPS = 1e-12

        def _dilate_pattern(adj_bool, mask_b):
            N = adj_bool.shape[0]

            def step(carry, n):
                row = jnp.take(carry, n, axis=0)
                nbi = row.astype(jnp.int32)
                num = jnp.sum(nbi)
                sf = jnp.where(num > T_DIL, (num + K_DIL - 1) // K_DIL, 1)
                rank = jnp.cumsum(nbi)
                rm = row & (rank % sf == 0)
                valid = (mask_b[n] != 0) & (num > 1)
                rm = jnp.where(valid, rm, False)
                keep = ~rm
                carry = carry.at[n].set(row & keep)
                carry = carry.at[:, n].set(carry[:, n] & keep)
                return (carry, None)
            out, _ = jax.lax.scan(step, adj_bool, jnp.arange(N))
            return out

        def _dilate(adj, mask):
            keep = jax.vmap(_dilate_pattern)(adj > 0, mask)
            return adj * keep.astype(adj.dtype)

        def _sage(x, adj, Wr, Wx, b, mf):
            deg = jnp.clip(jnp.sum(adj, axis=-1, keepdims=True), 1.0, None)
            agg = jnp.einsum('bij,bjd->bid', adj, x) / deg
            out = agg @ Wr + x @ Wx + b
            nrm = jnp.maximum(jnp.linalg.norm(out, axis=-1, keepdims=True), NORM_EPS)
            return out / nrm * mf[..., None]

        def _bn(x, g, b):
            m = jnp.mean(x, axis=(0, 1))
            v = jnp.var(x, axis=(0, 1))
            return (x - m) * jax.lax.rsqrt(v + BN_EPS) * g + b

        def _forward(x, adj, mask, Wr1, Wx1, b1, g1, be1, Wr2, Wx2, b2, g2, be2, Wr3, Wx3, b3, g3, be3, Wl, bl):
            mf = mask.astype(x.dtype)
            adj_d = _dilate(adj, mask)
            h1 = _bn(jax.nn.relu(_sage(x, adj_d, Wr1, Wx1, b1, mf)), g1, be1)
            h2 = _bn(jax.nn.relu(_sage(h1, adj_d, Wr2, Wx2, b2, mf)), g2, be2)
            h3 = _bn(jax.nn.relu(_sage(h2, adj_d, Wr3, Wx3, b3, mf)), g3, be3)
            xc = jnp.concatenate([h1, h2, h3], axis=-1) * mf[..., None]
            return (xc @ Wl + bl) * mf[..., None]
        return _forward(x, adj, mask, Wr1, Wx1, b1, g1, be1, Wr2, Wx2, b2, g2, be2, Wr3, Wx3, b3, g3, be3, Wl, bl)
    h = jnp.maximum(_layernorm(x, axis=-1), 0.0)
    x = x + _L0_gnn_ref(h, adj, nodemask, L0_gnn_Wr1, L0_gnn_Wx1, L0_gnn_b1, L0_gnn_g1, L0_gnn_be1, L0_gnn_Wr2, L0_gnn_Wx2, L0_gnn_b2, L0_gnn_g2, L0_gnn_be2, L0_gnn_Wr3, L0_gnn_Wx3, L0_gnn_b3, L0_gnn_g3, L0_gnn_be3, L0_gnn_Wl, L0_gnn_bl)
    return x

_drawn_inputs = setup_inputs


def setup_inputs(seed=0):
    import zlib

    import numpy as np

    out = dict(_drawn_inputs(seed))
    spreads = {'L0_gnn_b1': (0.0, 0.1),
     'L0_gnn_g1': (1.0, 0.2),
     'L0_gnn_be1': (0.0, 0.1),
     'L0_gnn_b2': (0.0, 0.1),
     'L0_gnn_g2': (1.0, 0.2),
     'L0_gnn_be2': (0.0, 0.1),
     'L0_gnn_b3': (0.0, 0.1),
     'L0_gnn_g3': (1.0, 0.2),
     'L0_gnn_be3': (0.0, 0.1),
     'L0_gnn_bl': (0.0, 0.1)}
    factors = {}
    for name, (base, spread) in spreads.items():
        noise = np.random.default_rng([zlib.crc32(name.encode()), seed]).standard_normal(out[name].shape)
        drawn = base * np.exp(spread * noise) if base else spread * noise
        out[name] = jnp.asarray(drawn.astype(out[name].dtype))
    for name, factor in factors.items():
        out[name] = (out[name] * factor).astype(out[name].dtype)
    return out
```

```python
from contextlib import ExitStack

import concourse.bass as bass
from concourse import mybir

F32, BF16, F16 = mybir.dt.float32, mybir.dt.bfloat16, mybir.dt.float16
F8, I32 = mybir.dt.float8e4, mybir.dt.int32
ALU, ACT, AX = mybir.AluOpType, mybir.ActivationFunctionType, mybir.AxisListType

P = 128
NB, N, D = 8, 1024, 128
NT = N // P
LAYERS = 3
BANK = 512

EDGE = 2048.0
SHIFT = 1024.0
NEVER = 4096.0
FAR = 9000.0
ALL = 1000.0
ROUND = 1.5 * 2.0 ** 23
SWEEPS = [3, 6, 6, 5, 4, 4, 5, 6]
STEPS = 9
GAP, FEW, HALF, SOME, CODE, PARITY, SMALL, HIT, EVEN = range(1, STEPS + 1)

SLOTS = 4
RING = 3
WZ = 3 * P + 1
ZROW = WZ + 1
BN_EPS, LN_EPS, NORM_EPS = 1e-5, 1e-5, 1e-12


def pieces(lo, hi):
    cuts = [lo] + [c for c in range(BANK, N, BANK) if lo < c < hi] + [hi]
    return list(zip(cuts[:-1], cuts[1:]))


def order():
    tasks = [("C", 0, b) for b in range(NB)]
    for i in range(NT):
        jobs = []
        if i:
            for b in range(NB + 1):
                if b < NB:
                    jobs.append(("V", i - 1, b))
                if b:
                    jobs += [("D", i - 1, b - 1), ("X", i - 1, b - 1)]
        if i + 1 < NT:
            jobs += [("C", i + 1, b) for b in range(NB)]
        if i == 1:
            jobs += [("H", 0, b) for b in range(NB)]
        tasks.append(("S", i, 0))
        per = -(-len(jobs) // (SWEEPS[i] + 1))
        for k in range(SWEEPS[i]):
            tasks.append(("W", i, k))
            tasks += jobs[:per]
            jobs = jobs[per:]
        tasks.append(("F", i, 0))
        tasks += jobs
        tasks += [("P", i, b) for b in range(NB)]
    for b in range(NB + 1):
        if b < NB:
            tasks.append(("V", NT - 1, b))
        if b:
            tasks += [("D", NT - 1, b - 1), ("X", NT - 1, b - 1)]
    return tasks


TASKS = order()
USES = [u for kind, i, b in TASKS if kind in "CPVDXH"
        for u in ((("L", i, b), ("M", i, b)) if kind == "D" and i else
                  (("L", i, b),) if kind == "D" else ((kind, i, b),))]
SLOT = {use: n % RING for n, use in enumerate(USES)}
BEFORE = {use: USES[n - RING] if n >= RING else None for n, use in enumerate(USES)}


def count(use):
    kind, i, b = use
    return (i - (kind == "M")) * NB + b + 1


def sweep_number(i, k):
    return sum(SWEEPS[:i]) + i + k


def build(nc, x, adj, nodemask, wr, wx, bias, gain, shift, wl, bl, out):
    with ExitStack() as ctx:
        def sb(name, shape, dt):
            return ctx.enter_context(nc.sbuf_tensor(name, shape, dt))

        def pb(name, shape, dt=F32):
            return ctx.enter_context(nc.psum_tensor(name, shape, dt))

        def sem(name):
            return ctx.enter_context(nc.semaphore(name))

        graph = sb("graph", [P, NT, NB, N], F8)
        codes = sb("codes", [P, 2 * NB * N], F16)
        ranks = codes[:, :].rearrange("p (q b m) -> p q b m", q=2, b=NB)
        ysum = codes[:, :].bitcast(F32).rearrange("p (b t d) -> p b t d", b=NB, t=NT)
        rT = sb("rT", [P, NB, N], F32)
        arena = sb("arena", [P, (SLOTS + 9) * N], F32)
        taken = [0]

        def cut(words, dt=F32):
            taken[0] += words
            piece = arena[:, taken[0] - words:taken[0]]
            return piece if dt == F32 else piece.bitcast(dt)

        stage = cut(SLOTS * N).rearrange("p (s j c) -> p s j c", s=SLOTS, j=NT)
        hit_rows = cut(4 * N, BF16).rearrange("p (k q m) -> p k q m", k=4, q=2)
        low_codes = cut(N, F16).rearrange("p (q m) -> p q m", q=2)
        diag_codes = cut(N, F16).rearrange("p (q m b) -> p q m b", q=2, b=NB)
        hit = cut(N // 2, BF16).rearrange("p (m b) -> p m b", b=NB)
        last_edge = cut(N // 2, BF16).rearrange("p (m b) -> p m b", b=NB)
        diag_low = cut(N, BF16).rearrange("p (q b c) -> p q b c", q=2, b=NB)
        diag_up = cut(N, BF16).rearrange("p (q b c) -> p q b c", q=2, b=NB)
        taken[0] = 0
        zo = cut(4 * N).rearrange("p (q t c) -> p q t c", q=2, t=NT)
        parts = cut(NT * ZROW, BF16).rearrange("p (q t c) -> p q t c", q=2, t=NT)
        rest = cut(N).rearrange("p (t d) -> p t d", t=NT)
        sage = cut(2 * N).rearrange("p (q t d) -> p q t d", q=2, t=NT)
        squares = cut(N // 2, BF16)
        part_sum = cut(4 * D).rearrange("p (q t d) -> p q t d", q=2, t=2)
        shift_wide = cut(2 * P).rearrange("p (q c) -> p q c", q=2)
        rowconst = cut(2 * D)
        wcur = cut(3 * D)
        wscaled = cut(3 * D)
        xin = sb("xin", [P, 2, NT, D], F32)
        kept_diag = sb("kept_diag", [P, 2, P], BF16)
        stair = sb("stair", [P, N], BF16)
        eye = sb("eye", [P, P], BF16)
        neg_eye = sb("neg_eye", [P, P], BF16)
        off_eye = sb("off_eye", [P, P], F16)
        low_mask = sb("low_mask", [P, P], F32)
        up_mask = sb("up_mask", [P, P], F32)
        eye32 = sb("eye32", [P, P], F32)
        pool_dot = sb("pool_dot", [1, 1], F32)
        ones = sb("ones", [P, 1], BF16)
        zeros = sb("zeros", [P, NB], BF16)
        mask_rows = sb("mask_rows", [NB * NT, P], I32)
        vectors = sb("vectors", [NB * NT + 2 * LAYERS, P], F32)
        columns = sb("columns", [P, NB * NT + 2 * LAYERS], F32)
        mask = columns[:, 0:NB * NT].rearrange("p (b t) -> p b t", b=NB)
        live = sb("live", [P, NB, NT], F32)
        left_right = sb("left_right", [P, 2, NB], F32)
        gap0, few_at, some_at, last_at = (sb(n, [P, NB], F32) for n in
                                          ("gap0", "few_at", "some_at", "last_at"))
        last_code = sb("last_code", [P, NB], F16)
        gap = sb("gap", [P, 2, NB], F32)
        few, half, some, parity = (sb(n, [P, NB], F32) for n in ("few", "half", "some", "parity"))
        code = sb("code", [P, NB], F16)
        small, even, changed = (sb(n, [P, NB], BF16) for n in ("small", "even", "changed"))
        flag = sb("flag", [1, 1], I32)
        edge_a, edge_b, left = (sb(n, [P, NB], F32) for n in ("edge_a", "edge_b", "left"))
        hit_at = sb("hit_at", [P, 4, 2, NB], F32)
        lnm, lnv = sb("lnm", [P, 2, NT], F32), sb("lnv", [P, 3, NT], F32)
        wraw = sb("wraw", [P, LAYERS, 3 * D], F32)
        bias_wide = sb("bias_wide", [P, LAYERS, 2 * D], F32)
        head_const = sb("head_const", [P, D], F32)
        degree = sb("degree", [P, 2, 2], F32)
        norms = sb("norms", [P, 4, NT], F32)
        moments = sb("moments", [P, 2, NB], F32)
        bn = sb("bn", [P, 10], F32)
        affine = sb("affine", [P, 2], F32)

        ring = pb("ring", [P, RING, 2 * BANK])
        counts = pb("counts", [P, BANK])
        spare = pb("spare", [P, BANK])
        removed = counts[:, 0:NB]
        agg_ps = ring[:, 0:2, :].rearrange("p s (k c) -> p s k c", k=2)
        turn_ps = ring[:, 2, :]
        prod_ps = [counts, spare]

        adj_in = [sem(f"adj_in{s}") for s in range(SLOTS)]
        x_in = [sem(f"x_in{s}") for s in range(2)]
        params_in, mask_in = sem("params_in"), sem("mask_in")
        consts_made, rows_ready = sem("consts_made"), sem("rows_ready")
        pool_step, cast_done, diag_codes_ready = sem("pool_step"), sem("cast_done"), sem("diag_codes_ready")
        columns_ps, columns_ready = sem("columns_ps"), sem("columns_ready")
        ps_ready = {k: sem(f"ps_ready_{k}") for k in "CPVLMXH"}
        ps_free = {k: sem(f"ps_free_{k}") for k in "CPVLMXH"}
        removed_ready = sem("removed_ready")
        setup_step, sweep_step = sem("setup_step"), sem("sweep_step")
        final_step, changed_ready, flag_ps, flag_ready = (
            sem(n) for n in ("final_step", "changed_ready", "flag_ps", "flag_ready"))
        more_step = [sem(f"more_step{i}") for i in range(NT)]
        more_removed = [sem(f"more_removed{i}") for i in range(NT)]
        hits_up, hits_low, kept_step = sem("hits_up"), sem("hits_low"), sem("kept_step")
        ln_sum, ln_centred, ln_squared, ln_var, ln_root, ln_scale, ln_done = (
            sem(n) for n in ("ln_sum", "ln_centred", "ln_squared", "ln_var", "ln_root", "ln_scale",
                             "ln_done"))
        prep_step, wide_ready, rowconst_ps = sem("prep_step"), sem("wide_ready"), sem("rowconst_ps")
        prod_ready, prod_free = sem("prod_ready"), sem("prod_free")
        top_ready, rest_ready, mid_ready, low_ready = (
            sem(n) for n in ("top_ready", "rest_ready", "mid_ready", "low_ready"))
        agg_ready, sage_step, sage_ready = sem("agg_ready"), sem("sage_step"), sem("sage_ready")
        squared, root_ready, norm_step, unit_ready = (
            sem(n) for n in ("squared", "root_ready", "norm_step", "unit_ready"))
        turn_ready, turned, moments_ready = sem("turn_ready"), sem("turned"), sem("moments_ready")
        bn_step, bn_var, bn_root, bn_wide, head_ps, head_const_ready, head_w = (
            sem(n) for n in ("bn_step", "bn_var", "bn_root", "bn_wide", "head_ps",
                             "head_const_ready", "head_w"))
        y_ps, y_added = sem("y_ps"), sem("y_added")
        start_step, last_step, xout_in, stored = (
            sem("start_step"), sem("last_step"), [sem(f"xout_in{s}") for s in range(2)], sem("stored"))
        out_ready = sem("out_ready")

        def slot(use):
            return ring[:, SLOT[use], :]

        def hits(kind, i, b):
            k = 0 if kind == "U" else 2
            return hit_rows[:, k, b % 2, :], hit_rows[:, k + 1, b % 2, :]

        block = ctx.enter_context(nc.Block())

        @block.sync
        def _(sp):
            sp.dma_start(mask_rows[:, :], nodemask.rearrange("b (t p) -> (b t) p", p=P)).then_inc(mask_in, 16)
            for l in range(LAYERS):
                r = NB * NT + l
                sp.dma_start(vectors[r:r + 1, :], gain[l].unsqueeze(0)).then_inc(params_in, 16)
                sp.dma_start(vectors[r + LAYERS:r + LAYERS + 1, :], shift[l].unsqueeze(0)).then_inc(params_in, 16)
            for n in range(NT * NB):
                i, b = divmod(n, NB)
                if n >= SLOTS:
                    sp.wait_ge(cast_done, n - SLOTS + 1)
                tiles = adj[b, i * P:N, i * P:(i + 1) * P].rearrange("(j p) c -> p j c", p=P)
                sp.dma_start(stage[:, n % SLOTS, 0:NT - i, :], tiles).then_inc(adj_in[n % SLOTS], 16)
                if n in (NB, NB + 1):
                    g = n - NB
                    sp.dma_start(xin[:, g, :, :], x[g].rearrange("(t p) d -> p t d", p=P)).then_inc(x_in[g], 16)
            for l in range(LAYERS):
                for k, w in enumerate((wr, wx, wl)):
                    src = w[l] if k < 2 else wl[l * D:(l + 1) * D, :]
                    sp.dma_start(wraw[:, l, k * D:(k + 1) * D], src).then_inc(params_in, 16)
                sp.dma_start(bias_wide[:, l, D:2 * D], bias[l].unsqueeze(0).broadcast_to([P, D])
                             ).then_inc(params_in, 16)
            sp.dma_start(head_const[:, :], bl.unsqueeze(0).broadcast_to([P, D])).then_inc(params_in, 16)
            for b in range(NB):
                if b < 2:
                    sp.wait_ge(ps_ready["H"], NB)
                else:
                    sp.wait_ge(out_ready, b - 1)
                    sp.wait_ge(stored, 16 * (b - 1))
                sp.dma_start(xin[:, b % 2, :, :], x[b].rearrange("(t p) d -> p t d", p=P)
                             ).then_inc(xout_in[b % 2], 16)
                if b >= 1:
                    sp.wait_ge(out_ready, b)
                    sp.dma_start(out[b - 1].rearrange("(t p) d -> p t d", p=P),
                                 xin[:, (b - 1) % 2, :, :]).then_inc(stored, 16)
            sp.wait_ge(out_ready, NB)
            sp.dma_start(out[NB - 1].rearrange("(t p) d -> p t d", p=P),
                         xin[:, (NB - 1) % 2, :, :]).then_inc(stored, 16)
            sp.wait_ge(stored, 16 * NB)

        @block.gpsimd
        def _(pool):
            made = 0
            for tile, value in ((eye[:, :], 0.0), (neg_eye[:, :], 0.0), (eye32[:, :], 0.0),
                                (off_eye[:, :], 1.0), (stair[:, :], 1.0), (low_mask[:, :], 1.0),
                                (up_mask[:, :], 1.0), (ones[:, :], 1.0), (zeros[:, :], 0.0),
                                (bias_wide[:, :, 0:D], 0.0)):
                made += 1
                pool.memset(tile, value).then_inc(pool_step, 1)
            pool.wait_ge(pool_step, made)

            def select(tile, op, fill, sign):
                return pool.affine_select(out=tile, in_=tile, compare_op=op, fill=fill, base=0,
                                          pattern=[[sign, P]], channel_multiplier=-sign)

            select(eye[:, :], ALU.not_equal, 1.0, 1).then_inc(consts_made, 1)
            select(neg_eye[:, :], ALU.not_equal, -1.0, 1).then_inc(consts_made, 1)
            select(eye32[:, :], ALU.not_equal, 1.0, 1).then_inc(consts_made, 1)
            select(off_eye[:, :], ALU.not_equal, 0.0, 1).then_inc(consts_made, 1)
            select(low_mask[:, :], ALU.is_ge, 0.0, -1).then_inc(consts_made, 1)
            select(up_mask[:, :], ALU.is_gt, 0.0, 1).then_inc(consts_made, 1)
            select(stair[:, 0:P], ALU.is_ge, 0.0, 1).then_inc(pool_step, 1)
            pool.wait_ge(pool_step, made + 1)
            select(stair[:, 0:P], ALU.not_equal, EDGE, 1).then_inc(consts_made, 1)
            pool.wait_ge(consts_made, 7)
            step = made + 1

            def cast(i, b, step):
                n = i * NB + b
                pool.wait_ge(adj_in[n % SLOTS], 16 * (n // SLOTS + 1))
                diag = stage[:, n % SLOTS, 0, :]
                if i >= 2:
                    pool.wait_ge(ps_ready["P"], (i - 2) * NB + b + 1)
                pool.tensor_tensor(diag_low[:, i % 2, b, :], diag, low_mask[:, :], ALU.mult).then_inc(pool_step, 1)
                pool.tensor_tensor(diag_up[:, i % 2, b, :], diag, up_mask[:, :], ALU.mult).then_inc(pool_step, 1)
                pool.wait_ge(pool_step, step + 2)
                if i + 1 < NT:
                    pool.tensor_copy(graph[:, i + 1:NT, b, i * P:(i + 1) * P],
                                     stage[:, n % SLOTS, 1:NT - i, :], saturate=False).then_inc(cast_done, 1)
                else:
                    pool.memset(pool_dot[:, :], 0.0).then_inc(cast_done, 1)
                return step + 2

            def norm_input(b):
                pool.wait_ge(ln_sum, b + 1)
                xc = xin[:, b % 2, :, :]
                xsq = rT[:, b, :].rearrange("p (t d) -> p t d", t=NT)
                pool.tensor_tensor(xc, xc,
                                   lnm[:, b % 2, :].unsqueeze(2).broadcast_to([P, NT, D]),
                                   ALU.subtract).then_inc(ln_centred, 1)
                pool.wait_ge(ln_centred, b + 1)
                pool.tensor_tensor(xsq, xc, xc, ALU.mult).then_inc(ln_squared, 1)
                pool.wait_ge(ln_scale, b + 1)
                pool.wait_ge(ln_squared, b + 1)
                pool.tensor_tensor(xc, xc,
                                   lnv[:, 2, :].unsqueeze(2).broadcast_to([P, NT, D]),
                                   ALU.mult).then_inc(ln_done, 1)

            for b in range(NB):
                step = cast(0, b, step)
            for b in range(NB):
                step = cast(1, b, step)
            for kind, i, b in TASKS:
                if kind == "C" and b == NB - 1:
                    pool.wait_ge(ps_free["C"], (i + 1) * NB)
                    d = ranks[:, i % 2, :, 0:P]
                    pool.tensor_tensor(d, d, off_eye[:, :].unsqueeze(1).broadcast_to([P, NB, P]),
                                       ALU.mult).then_inc(pool_step, 1)
                    step += 1
                    pool.wait_ge(pool_step, step)
                    if i >= 2:
                        pool.wait_ge(final_step, (i - 1) * 7)
                    pool.tensor_copy(diag_codes[:, i % 2, :, :].rearrange("p m b -> p b m"), d
                                     ).then_inc(diag_codes_ready, 1)
                elif kind == "P" and i + 2 < NT:
                    step = cast(i + 2, b, step)
                elif kind == "H":
                    norm_input(b)

            def split(l, b):
                n = l * NB + b
                pool.wait_ge(top_ready, n + 1)
                pool.tensor_tensor(rest[:, :, :], zo[:, b % 2, :, 0:D], parts[:, b % 2, :, 0:D],
                                   ALU.subtract).then_inc(rest_ready, 1)
                pool.wait_ge(mid_ready, n + 1)
                pool.tensor_tensor(parts[:, b % 2, :, 2 * D:3 * D], rest[:, :, :],
                                   parts[:, b % 2, :, D:2 * D], ALU.subtract).then_inc(low_ready, 1)
                pool.wait_ge(low_ready, n + 1)

            pool.wait_ge(start_step, 1)
            pool.memset(parts[:, :, :, 3 * D:WZ], 1.0).then_inc(pool_step, 1)
            pool.wait_ge(pool_step, step + 1)
            with pool.Fori(0, LAYERS) as l:
                for b in range(NB):
                    split(l, b)

        @block.vector
        def _(dve):
            dve.wait_ge(mask_in, 16)
            dve.tensor_copy(vectors[0:NB * NT, :], mask_rows[:, :]).then_inc(rows_ready, 1)
            dve.wait_ge(columns_ps, 1)
            dve.tensor_copy(columns[:, :], spare[:, 0:NB * NT + 2 * LAYERS]).then_inc(columns_ready, 1)
            dve.wait_ge(columns_ready, 1)
            dve.tensor_scalar(live[:, :, :], mask, 0.0, None, ALU.not_equal).then_inc(columns_ready, 1)
            dve.wait_ge(columns_ready, 2)

            def setup(i):
                n = i * 10
                dve.wait_ge(removed_ready, sweep_number(i, 0) + 1)
                dve.tensor_copy(left_right[:, :, :], counts[:, NB:3 * NB].rearrange("p (k b) -> p k b", k=2)
                                ).then_inc(setup_step, 1)
                dve.wait_ge(setup_step, n + 1)
                l0, u = left_right[:, 0, :], left_right[:, 1, :]
                alive = live[:, :, i]
                dve.tensor_tensor(gap0[:, :], u, l0, ALU.subtract).then_inc(setup_step, 1)
                dve.scalar_tensor_tensor(few_at[:, :], u, FAR - 5.0, alive, ALU.add, ALU.mult).then_inc(setup_step, 1)
                dve.scalar_tensor_tensor(some_at[:, :], u, FAR - 0.5, alive, ALU.add, ALU.mult).then_inc(setup_step, 1)
                dve.tensor_scalar(last_at[:, :], u, -1.0, FAR - SHIFT + 1.0, ALU.mult, ALU.add).then_inc(setup_step, 1)
                dve.tensor_scalar(last_code[:, :], u, SHIFT - 1.0, None, ALU.add).then_inc(setup_step, 1)
                dve.wait_ge(setup_step, n + 6)
                dve.tensor_scalar(gap0[:, :], gap0[:, :], 0.5, 0.25, ALU.mult, ALU.add).then_inc(setup_step, 1)
                dve.tensor_scalar(few_at[:, :], few_at[:, :], -FAR, None, ALU.add).then_inc(setup_step, 1)
                dve.tensor_scalar(some_at[:, :], some_at[:, :], -FAR, None, ALU.add).then_inc(setup_step, 1)
                dve.wait_ge(diag_codes_ready, i + 1)
                dve.tensor_tensor(last_edge[:, :, :], diag_codes[:, i % 2, :, :],
                                  last_code[:, :].unsqueeze(1).broadcast_to([P, P, NB]),
                                  ALU.is_equal).then_inc(setup_step, 1)
                dve.wait_ge(setup_step, n + 10)

            def sweep(i, gap_now, done, at, with_hits):
                dve.scalar_tensor_tensor(gap_now, removed, 0.5, gap0[:, :], ALU.mult, ALU.add).then_inc(done, 1)
                dve.wait_ge(done, at + GAP)
                dve.tensor_tensor(few[:, :], gap_now, few_at[:, :], ALU.is_ge).then_inc(done, 1)
                dve.tensor_scalar(half[:, :], gap_now, ROUND, ROUND - SHIFT + 1.0, ALU.add,
                                  ALU.subtract).then_inc(done, 1)
                dve.tensor_tensor(some[:, :], gap_now, some_at[:, :], ALU.is_lt).then_inc(done, 1)
                dve.wait_ge(done, at + HALF)
                dve.scalar_tensor_tensor(code[:, :], few[:, :], NEVER, half[:, :], ALU.mult,
                                         ALU.max).then_inc(done, 1)
                dve.tensor_tensor(parity[:, :], gap_now, half[:, :], ALU.subtract).then_inc(done, 1)
                dve.wait_ge(done, at + SOME)
                dve.tensor_tensor(small[:, :], few[:, :], some[:, :], ALU.mult).then_inc(done, 1)
                dve.wait_ge(done, at + CODE)
                if with_hits:
                    dve.tensor_tensor(hit[:, :, :], diag_codes[:, i % 2, :, :],
                                      code[:, :].unsqueeze(1).broadcast_to([P, P, NB]),
                                      ALU.is_equal).then_inc(done, 1)
                else:
                    dve.tensor_tensor(changed[:, :], gap[:, 0, :], gap[:, 1, :], ALU.not_equal).then_inc(done, 1)
                dve.wait_ge(done, at + PARITY)
                dve.scalar_tensor_tensor(even[:, :], parity[:, :], 1.0 - SHIFT, few[:, :], ALU.is_gt,
                                         ALU.is_gt).then_inc(done, 1)

            def final(i):
                g = sweep_number(i, SWEEPS[i])
                dve.wait_ge(removed_ready, g + 1)
                dve.wait_ge(sweep_step, STEPS * g)
                sweep(i, gap[:, SWEEPS[i] % 2, :], sweep_step, STEPS * g, False)
                dve.wait_ge(flag_ps, i + 1)
                dve.tensor_reduce(flag[:, :], spare[0:1, 0:NB], AX.X, ALU.max).then_inc(flag_ready, 1)
                dve.wait_ge(flag_ready, i + 1)
                more = dve.value_load(flag[0:1, 0:1], min_val=0, max_val=P)
                with dve.If(more > 0):
                    dve.wait_ge(sweep_step, STEPS * (g + 1))
                    with dve.Fori(0, P) as k:
                        sweep(i, gap[:, 0, :], more_step[i], k * STEPS, True)
                        dve.wait_ge(more_step[i], k * STEPS + EVEN)
                        dve.wait_ge(more_removed[i], k + 1)
                    sweep(i, gap[:, 0, :], more_step[i], P * STEPS, False)
                    dve.wait_ge(more_step[i], (P + 1) * STEPS)
                n = i * 7
                dve.wait_ge(sweep_step, STEPS * (g + 1))
                up_code, up_from, low_code, low_from = (hit_at[:, k, i % 2, :] for k in range(4))
                dve.tensor_tensor(edge_a[:, :], even[:, :], last_at[:, :], ALU.mult).then_inc(final_step, 1)
                dve.tensor_tensor(left[:, :], left_right[:, 0, :], removed, ALU.subtract).then_inc(final_step, 1)
                dve.tensor_copy(up_code, code[:, :]).then_inc(final_step, 1)
                dve.wait_ge(final_step, n + 3)
                dve.scalar_tensor_tensor(edge_b[:, :], small[:, :], FAR - ALL, edge_a[:, :], ALU.mult,
                                         ALU.add).then_inc(final_step, 1)
                dve.tensor_tensor(low_code, up_code, left[:, :], ALU.add).then_inc(final_step, 1)
                dve.wait_ge(final_step, n + 5)
                dve.tensor_scalar(up_from, edge_b[:, :], -1.0, FAR, ALU.mult, ALU.add).then_inc(final_step, 1)
                dve.wait_ge(final_step, n + 6)
                dve.tensor_tensor(low_from, up_from, left[:, :], ALU.add).then_inc(final_step, 1)
                dve.wait_ge(final_step, n + 7)

            def mark(kind, i, b):
                n = i * NB + b
                width = N - i * P if kind == "U" else (i + 1) * P
                if kind == "U":
                    src, done, k = ranks[:, i % 2, b, 0:width], hits_up, 0
                    reader = ps_ready["P"]
                    if n >= 2:
                        dve.wait_ge(reader, n - 1)
                else:
                    src, done, k = low_codes[:, b % 2, 0:width], hits_low, 2
                    dve.wait_ge(ps_free["V"], n + 1)
                    if b >= 2:
                        dve.wait_ge(ps_ready["L" if not i else "M"], n - 1 - (NB if i else 0))
                    elif i:
                        before = n - 2
                        pi = before // NB
                        dve.wait_ge(ps_ready["L" if not pi else "M"], before + 1 - (NB if pi else 0))
                one, two = hits(kind, i, b)
                dve.tensor_scalar(one[:, 0:width], src, hit_at[:, k, i % 2, b:b + 1], None,
                                  ALU.is_equal).then_inc(done, 1)
                dve.tensor_scalar(two[:, 0:width], src, hit_at[:, k + 1, i % 2, b:b + 1], None,
                                  ALU.is_ge).then_inc(done, 1)

            for kind, i, b in TASKS:
                if kind == "S":
                    setup(i)
                elif kind == "W":
                    g = sweep_number(i, b)
                    dve.wait_ge(removed_ready, g + 1)
                    if g:
                        dve.wait_ge(sweep_step, STEPS * g)
                    sweep(i, gap[:, b % 2, :], sweep_step, STEPS * g, True)
                elif kind == "F":
                    final(i)
                elif kind == "P":
                    mark("U", i, b)
                elif kind == "V":
                    mark("L", i, b)
                elif kind == "X":
                    dve.wait_ge(ps_ready["X"], i * NB + b + 1)
                    dve.tensor_scalar(graph[:, i, b, i * P:(i + 1) * P], slot(("X", i, b))[:, 0:P], 0.0,
                                      None, ALU.is_gt, saturate=False).then_inc(ps_free["X"], 1)
                elif kind == "H":
                    dve.wait_ge(x_in[b % 2], 16 * (b // 2 + 1))
                    if b >= 2:
                        dve.wait_ge(ln_centred, b - 1)
                    if b:
                        dve.wait_ge(ln_var, 3 * b)
                    dve.tensor_reduce(lnv[:, 0, :], xin[:, b % 2, :, :], AX.X, ALU.add).then_inc(ln_var, 1)
                    dve.wait_ge(ln_var, 3 * b + 1)
                    dve.tensor_scalar(lnm[:, b % 2, :], lnv[:, 0, :], 1.0 / D, None, ALU.mult).then_inc(ln_sum, 1)
                    dve.wait_ge(ln_squared, b + 1)
                    dve.tensor_reduce(lnv[:, 0, :], rT[:, b, :].rearrange("p (t d) -> p t d", t=NT), AX.X, ALU.add).then_inc(ln_var, 1)
                    dve.wait_ge(ln_var, 3 * b + 2)
                    if b:
                        dve.wait_ge(ln_scale, b)
                    dve.tensor_scalar(lnv[:, 1, :], lnv[:, 0, :], 1.0 / D, LN_EPS, ALU.mult, ALU.add).then_inc(ln_var, 1)
                    dve.wait_ge(ln_root, b + 1)
                    if b:
                        dve.wait_ge(ln_done, b)
                    dve.reciprocal(lnv[:, 2, :], lnv[:, 1, :]).then_inc(ln_scale, 1)

            for k in "CPVLXH":
                dve.wait_ge(ps_free[k], NB if k == "H" else NT * NB)
            dve.wait_ge(ps_free["M"], (NT - 1) * NB)
            dve.wait_ge(params_in, 16 * (6 + 4 * LAYERS + 1))
            dve.memset(affine[:, 0:1], 1.0).then_inc(prep_step, 1)
            dve.memset(affine[:, 1:2], 0.0).then_inc(prep_step, 1)
            dve.memset(ysum[:, :, :, :].rearrange("p b t d -> p (b t d)"), 0.0).then_inc(start_step, 1)
            dve.wait_ge(start_step, 1)
            dve.wait_ge(prep_step, 2)

            def products(l, b):
                for k in range(NT // 2):
                    n = (l * NB + b) * 4 + k
                    dve.wait_ge(prod_ready, n + 1)
                    dve.tensor_tensor(zo[:, b % 2, 2 * k:2 * k + 2, :],
                                      prod_ps[k % 2][:, :].rearrange("p (t c) -> p t c", t=2),
                                      rowconst[:, :].unsqueeze(1).broadcast_to([P, 2, 2 * D]),
                                      ALU.add).then_inc(prod_free, 1)

            def combine(l, b):
                for k in range(4):
                    n = (l * NB + b) * 4 + k
                    dve.wait_ge(agg_ready, n + 1)
                    ps = agg_ps[:, k % 2, :, :]
                    dve.tensor_scalar(degree[:, 0, :], ps[:, :, 3 * D], 1.0, None, ALU.max).then_inc(sage_step, 1)
                    dve.tensor_reduce(part_sum[:, k % 2, :, :], ps[:, :, 0:3 * D].rearrange(
                        "p t (s d) -> p t d s", s=3), AX.X, ALU.add).then_inc(sage_step, 1)
                    dve.wait_ge(sage_step, 3 * n + 1)
                    dve.reciprocal(degree[:, 1, :], degree[:, 0, :]).then_inc(sage_step, 1)
                    dve.wait_ge(sage_step, 3 * n + 3)
                    for h in range(2):
                        t = 2 * k + h
                        dve.scalar_tensor_tensor(sage[:, b % 2, t, :], part_sum[:, k % 2, h, :],
                                                 degree[:, 1, h:h + 1], zo[:, b % 2, t, D:2 * D],
                                                 ALU.mult, ALU.add).then_inc(sage_ready, 1)
                    dve.wait_ge(sage_ready, 2 * (n + 1))

            def unit(l, b):
                n = l * NB + b
                dve.wait_ge(root_ready, n + 1)
                dve.tensor_scalar(norms[:, 2, :], norms[:, 1, :], NORM_EPS, None, ALU.max).then_inc(norm_step, 1)
                dve.wait_ge(norm_step, 3 * n + 1)
                dve.reciprocal(norms[:, 3, :], norms[:, 2, :]).then_inc(norm_step, 1)
                dve.wait_ge(norm_step, 3 * n + 2)
                dve.tensor_tensor(norms[:, 3, :], norms[:, 3, :], mask[:, b, :], ALU.mult).then_inc(norm_step, 1)
                dve.wait_ge(norm_step, 3 * n + 3)
                dve.tensor_tensor(sage[:, b % 2, :, :], sage[:, b % 2, :, :],
                                  norms[:, 3, :].unsqueeze(2).broadcast_to([P, NT, D]),
                                  ALU.mult).then_inc(unit_ready, 1)
                dve.wait_ge(unit_ready, n + 1)

            PREP, BN = 2, 8
            with dve.Fori(0, LAYERS) as l:
                at = 2 + l * PREP
                lw = wraw[:, bass.ds(l, 1), :].rearrange("p a c -> p (a c)")
                dve.tensor_copy(wcur[:, :], lw).then_inc(prep_step, 1)
                dve.tensor_copy(shift_wide[:, 0, :], affine[:, 1:2].broadcast_to([P, P])).then_inc(wide_ready, 1)
                dve.wait_ge(prep_step, at + 1)
                dve.tensor_scalar(wscaled[:, 0:2 * D], wcur[:, 0:2 * D], affine[:, 0:1], None, ALU.mult
                                  ).then_inc(wide_ready, 1)
                dve.wait_ge(rowconst_ps, l + 1)
                bw = bias_wide[:, bass.ds(l, 1), :].rearrange("p a c -> p (a c)")
                dve.tensor_tensor(rowconst[:, :], prod_ps[0][:, 0:2 * D], bw, ALU.add).then_inc(prep_step, 1)
                dve.wait_ge(prep_step, at + PREP)
                products(l, 0)
                products(l, 1)
                for b in range(NB):
                    combine(l, b)
                    if b + 2 < NB:
                        products(l, b + 2)
                    unit(l, b)
                c = l * BN
                dve.wait_ge(moments_ready, 2 * NB * (l + 1))
                dve.tensor_reduce(bn[:, 0:2], moments[:, :, :], AX.X, ALU.add).then_inc(bn_step, 1)
                dve.wait_ge(bn_step, c + 1)
                dve.tensor_scalar(bn[:, 2:4], bn[:, 0:2], 1.0 / (NB * N), None, ALU.mult).then_inc(bn_step, 1)
                dve.wait_ge(bn_step, c + 2)
                dve.tensor_tensor(bn[:, 4:5], bn[:, 2:3], bn[:, 2:3], ALU.mult).then_inc(bn_step, 1)
                dve.wait_ge(bn_step, c + 3)
                dve.tensor_tensor(bn[:, 5:6], bn[:, 3:4], bn[:, 4:5], ALU.subtract).then_inc(bn_step, 1)
                dve.wait_ge(bn_step, c + 4)
                dve.tensor_scalar(bn[:, 6:7], bn[:, 5:6], 0.0, BN_EPS, ALU.max, ALU.add).then_inc(bn_var, 1)
                dve.wait_ge(bn_root, l + 1)
                dve.reciprocal(bn[:, 8:9], bn[:, 7:8]).then_inc(bn_step, 1)
                dve.wait_ge(bn_step, c + 5)
                gcol = columns[:, bass.ds(l + NB * NT, 1)]
                bcol = columns[:, bass.ds(l + NB * NT + LAYERS, 1)]
                dve.tensor_tensor(affine[:, 0:1], gcol, bn[:, 8:9], ALU.mult).then_inc(bn_step, 1)
                dve.wait_ge(bn_step, c + 6)
                dve.tensor_tensor(bn[:, 4:5], bn[:, 2:3], affine[:, 0:1], ALU.mult).then_inc(bn_step, 1)
                dve.wait_ge(bn_step, c + 7)
                dve.tensor_tensor(affine[:, 1:2], bcol, bn[:, 4:5], ALU.subtract).then_inc(bn_step, 1)
                dve.wait_ge(bn_step, c + 8)
                dve.tensor_copy(shift_wide[:, 1, :], affine[:, 1:2].broadcast_to([P, P])).then_inc(bn_wide, 1)
                dve.tensor_scalar(wscaled[:, 2 * D:3 * D], wcur[:, 2 * D:3 * D], affine[:, 0:1], None,
                                  ALU.mult).then_inc(head_w, 1)
                dve.wait_ge(head_ps, l + 1)
                dve.tensor_tensor(head_const[:, :], head_const[:, :], prod_ps[0][:, 0:D], ALU.add
                                  ).then_inc(head_const_ready, 1)
                for b in range(NB):
                    for h in range(2):
                        n = (l * NB + b) * 2 + h
                        dve.wait_ge(y_ps, n + 1)
                        dve.tensor_tensor(ysum[:, b, 4 * h:4 * h + 4, :], ysum[:, b, 4 * h:4 * h + 4, :],
                                          prod_ps[(b * 2 + h + 1) % 2][:, :].rearrange("p (t d) -> p t d", t=4),
                                          ALU.add).then_inc(y_added, 1)
                dve.wait_ge(y_added, (l + 1) * 2 * NB)
            for b in range(NB):
                y = ysum[:, b, :, :]
                dve.tensor_tensor(y, y, head_const[:, :].unsqueeze(1).broadcast_to([P, NT, D]), ALU.add
                                  ).then_inc(last_step, 1)
                dve.wait_ge(last_step, 2 * b + 1)
                dve.tensor_tensor(y, y, mask[:, b, :].unsqueeze(2).broadcast_to([P, NT, D]), ALU.mult
                                  ).then_inc(last_step, 1)
                dve.wait_ge(last_step, 2 * b + 2)
                dve.wait_ge(xout_in[b % 2], 16 * (b // 2 + 1))
                dve.tensor_tensor(xin[:, b % 2, :, :], xin[:, b % 2, :, :], y, ALU.add).then_inc(out_ready, 1)

        @block.scalar
        def _(act):
            for kind, i, b in TASKS:
                if kind == "C":
                    use = ("C", i, b)
                    act.wait_ge(ps_ready["C"], count(use))
                    if i >= 2:
                        act.wait_ge(hits_up, 2 * ((i - 2) * NB + b + 1))
                    act.activation(ranks[:, i % 2, b, 0:N - i * P], slot(use)[:, 0:N - i * P], ACT.Copy,
                                   bias=-SHIFT).then_inc(ps_free["C"], 1)
                elif kind == "P":
                    use = ("P", i, b)
                    act.wait_ge(ps_ready["P"], count(use))
                    act.activation(graph[:, i, b, i * P:N], slot(use)[:, 0:N - i * P], ACT.Copy,
                                   saturate=False).then_inc(ps_free["P"], 1)
                elif kind == "V":
                    use = ("V", i, b)
                    act.wait_ge(ps_ready["V"], count(use))
                    n = count(use)
                    if n > 2:
                        act.wait_ge(hits_low, 2 * (n - 2))
                    act.activation(low_codes[:, b % 2, 0:(i + 1) * P], slot(use)[:, 0:(i + 1) * P], ACT.Copy,
                                   bias=-SHIFT).then_inc(ps_free["V"], 1)
                elif kind == "D":
                    use = ("L", i, b)
                    act.wait_ge(ps_ready["L"], count(use))
                    n = count(use)
                    if n > 2:
                        act.wait_ge(ps_ready["X"], n - 2)
                    act.activation(kept_diag[:, b % 2, :], slot(use)[:, i * P:(i + 1) * P], ACT.Copy
                                   ).then_inc(ps_free["L"] if not i else kept_step, 1)
                    if i:
                        act.activation(graph[:, i, b, 0:i * P], slot(use)[:, 0:i * P], ACT.Copy,
                                       saturate=False).then_inc(ps_free["L"], 1)
                        use = ("M", i, b)
                        act.wait_ge(ps_ready["M"], count(use))
                        act.activation(graph[:, 0:i, b, i * P:(i + 1) * P],
                                       slot(use)[:, 0:i * P].rearrange("p (j c) -> p j c", j=i), ACT.Copy,
                                       saturate=False).then_inc(ps_free["M"], 1)
                elif kind == "H":
                    act.wait_ge(ln_var, 3 * b + 3)
                    act.activation(lnv[:, 1, :], lnv[:, 1, :], ACT.Sqrt).then_inc(ln_root, 1)
                    act.wait_ge(ps_ready["H"], b + 1)
                    act.activation(rT[:, b, :], slot(("H", 0, b)), ACT.Relu).then_inc(ps_free["H"], 1)
                    if b + 2 < NB:
                        act.dma_start(xin[:, b % 2, :, :], x[b + 2].rearrange("(t p) d -> p t d", p=P)
                                      ).then_inc(x_in[b % 2], 16)

            def top(l, b):
                act.wait_ge(prod_free, (l * NB + b + 1) * 4)
                act.activation(parts[:, b % 2, :, 0:D], zo[:, b % 2, :, 0:D], ACT.Copy).then_inc(top_ready, 1)

            def middle(l, b):
                act.wait_ge(rest_ready, l * NB + b + 1)
                act.activation(parts[:, b % 2, :, D:2 * D], rest[:, :, :], ACT.Copy).then_inc(mid_ready, 1)

            def lengths(l, b):
                n = l * NB + b
                for t in range(NT):
                    if t % 2 == 0:
                        act.wait_ge(sage_ready, n * NT + t + 2)
                    act.activation(squares[:, t * D:(t + 1) * D], sage[:, b % 2, t, :], ACT.Square,
                                   accum_out=norms[:, 0, t:t + 1]).then_inc(squared, 1)
                act.wait_ge(squared, (n + 1) * NT)
                act.activation(norms[:, 1, :], norms[:, 0, :], ACT.Sqrt).then_inc(root_ready, 1)

            def turn_out(l, b):
                n = l * NB + b
                act.wait_ge(turn_ready, n + 1)
                act.activation(rT[:, b, :], turn_ps, ACT.Relu, accum_out=moments[:, 0, b:b + 1]
                               ).then_inc(moments_ready, 1)
                act.wait_ge(moments_ready, 2 * n + 1)
                act.activation(squares, rT[:, b, :], ACT.Square, accum_out=moments[:, 1, b:b + 1]
                               ).then_inc(moments_ready, 1)
                act.wait_ge(moments_ready, 2 * n + 2)

            act.wait_ge(pool_step, 10 + 1 + 2 * NT * NB + NT + 1)
            with act.Fori(0, LAYERS) as l:
                top(l, 0)
                middle(l, 0)
                top(l, 1)
                middle(l, 1)
                for b in range(NB):
                    lengths(l, b)
                    if b + 2 < NB:
                        top(l, b + 2)
                    if b:
                        turn_out(l, b - 1)
                    if b + 2 < NB:
                        middle(l, b + 2)
                turn_out(l, NB - 1)
                act.wait_ge(bn_var, l + 1)
                act.activation(bn[:, 7:8], bn[:, 6:7], ACT.Sqrt).then_inc(bn_root, 1)

        @block.tensor
        def _(pe):
            def mm(out_, lhsT, rhs, start, stop):
                return pe.matmul(out_, lhsT, rhs, start=start, stop=stop)

            pe.wait_ge(consts_made, 7)
            pe.wait_ge(rows_ready, 1)
            pe.wait_ge(params_in, 16 * 2 * LAYERS)
            nv = NB * NT + 2 * LAYERS
            mm(spare[:, 0:nv], vectors[:, :], eye32[0:nv, 0:nv], True, True).then_inc(columns_ps, 1)

            def ready_slot(use):
                old = BEFORE[use]
                if old:
                    pe.wait_ge(ps_free[old[0]], count(old))

            def original(i, j, b):
                return diag_low[:, i % 2, b, :] if i == j else graph[:, j, b, i * P:(i + 1) * P]

            def prefix(ps, tiles, width):
                for first, (at, tile) in enumerate(tiles):
                    for lo, hi in pieces(at, width):
                        last = mm(ps[:, lo:hi], tile, stair[:, lo - at:hi - at], first == 0,
                                  at + P >= min(width, (lo // BANK + 1) * BANK))
                return last

            def minus(ps, marks, width, stop):
                for n, row in enumerate(marks):
                    for lo, hi in pieces(0, width):
                        last = mm(ps[:, lo:hi], neg_eye[:, :], row[:, lo:hi], False, stop and n == 1)
                return last

            def upper_ranks(i, b):
                use = ("C", i, b)
                ready_slot(use)
                pe.wait_ge(cast_done, i * NB + b + 1)
                prefix(slot(use), [((j - i) * P, original(i, j, b)) for j in range(i, NT)],
                       N - i * P).then_inc(ps_ready["C"], 1)

            def block_counts(i):
                pe.wait_ge(cast_done, (i + 1) * NB)
                if i:
                    pe.wait_ge(ps_free["P"], i * NB)
                    pe.wait_ge(final_step, i * 7)
                mm(removed, eye[:, :], zeros[:, :], True, False)
                for b in range(NB):
                    col = counts[:, NB + b:NB + b + 1]
                    for j in range(i):
                        mm(col, graph[:, j, b, i * P:(i + 1) * P], ones[:, :], False, False)
                    mm(col, diag_up[:, i % 2, b, :], ones[:, :], False, False)
                    col = counts[:, 2 * NB + b:2 * NB + b + 1]
                    for j in range(i, NT):
                        last = mm(col, original(i, j, b), ones[:, :], False, j == NT - 1 and b == NB - 1)
                last.then_inc(removed_ready, 1)

            def count_removed(i, done, at):
                pe.wait_ge(done, at)
                for b in range(NB):
                    mm(removed[:, b:b + 1], diag_up[:, i % 2, b, :], small[:, b:b + 1], b == 0, False)
                for b in range(NB):
                    mm(removed[:, b:b + 1], last_edge[:, :, b], even[:, b:b + 1], False, False)
                for b in range(NB):
                    last = mm(removed[:, b:b + 1], hit[:, :, b], ones[:, :], False, b == NB - 1)
                return last

            def test(i):
                g = sweep_number(i, SWEEPS[i])
                pe.wait_ge(sweep_step, STEPS * g + HIT)
                if i:
                    pe.wait_ge(flag_ready, i)
                pe.matmul(spare[0:1, 0:NB], ones[:, :], changed[:, :], start=True, stop=True).then_inc(flag_ps, 1)
                pe.wait_ge(flag_ready, i + 1)
                more = pe.value_load(flag[0:1, 0:1], min_val=0, max_val=P)
                with pe.If(more > 0):
                    with pe.Fori(0, P) as k:
                        count_removed(i, more_step[i], (k + 1) * STEPS).then_inc(more_removed[i], 1)

            def rows_after(i, b):
                use = ("P", i, b)
                ready_slot(use)
                ps, width = slot(use), N - i * P
                for j in range(i, NT):
                    at = (j - i) * P
                    mm(ps[:, at:at + P], original(i, j, b), eye[:, :], at % BANK == 0, False)
                pe.wait_ge(hits_up, 2 * (i * NB + b + 1))
                minus(ps, hits("U", i, b), width, True).then_inc(ps_ready["P"], 1)

            def lower_ranks(i, b):
                use = ("V", i, b)
                ready_slot(use)
                pe.wait_ge(ps_free["P"], i * NB + b + 1)
                prefix(slot(use), [(j * P, graph[:, j, b, i * P:(i + 1) * P]) for j in range(i + 1)],
                       (i + 1) * P).then_inc(ps_ready["V"], 1)

            def kept(i, b):
                use = ("L", i, b)
                ready_slot(use)
                ps, width = slot(use), (i + 1) * P
                pe.wait_ge(hits_low, 2 * (i * NB + b + 1))
                for j in range(i + 1):
                    mm(ps[:, j * P:(j + 1) * P], graph[:, j, b, i * P:(i + 1) * P], eye[:, :],
                       j * P % BANK == 0, False)
                minus(ps, hits("L", i, b), width, True).then_inc(ps_ready["L"], 1)
                if i:
                    use = ("M", i, b)
                    ready_slot(use)
                    ps = slot(use)
                    for j in range(i):
                        part = ps[:, j * P:(j + 1) * P]
                        mm(part, eye[:, :], graph[:, j, b, i * P:(i + 1) * P], j * P % BANK == 0, False)
                        for n, row in enumerate(hits("L", i, b)):
                            last = mm(part, row[:, j * P:(j + 1) * P], neg_eye[:, :], False,
                                      n == 1 and (j == i - 1 or (j + 1) * P % BANK == 0))
                    last.then_inc(ps_ready["M"], 1)

            def diagonal(i, b):
                use = ("X", i, b)
                ready_slot(use)
                if i:
                    pe.wait_ge(kept_step, (i - 1) * NB + b + 1)
                else:
                    pe.wait_ge(ps_free["L"], b + 1)
                tile = kept_diag[:, b % 2, :]
                mm(slot(use)[:, 0:P], tile, eye[:, :], True, False)
                mm(slot(use)[:, 0:P], eye[:, :], tile, False, True).then_inc(ps_ready["X"], 1)

            for kind, i, b in TASKS:
                if kind == "C":
                    upper_ranks(i, b)
                elif kind == "S":
                    block_counts(i)
                elif kind == "W":
                    g = sweep_number(i, b)
                    count_removed(i, sweep_step, STEPS * (g + 1)).then_inc(removed_ready, 1)
                elif kind == "F":
                    test(i)
                elif kind == "P":
                    rows_after(i, b)
                elif kind == "V":
                    lower_ranks(i, b)
                elif kind == "D":
                    kept(i, b)
                elif kind == "X":
                    diagonal(i, b)
                elif kind == "H":
                    use = ("H", 0, b)
                    ready_slot(use)
                    pe.wait_ge(ln_done, b + 1)
                    for t in range(NT):
                        last = pe.transpose(slot(use)[:, t * P:(t + 1) * P], xin[:, b % 2, t, :], eye32[:, :])
                    last.then_inc(ps_ready["H"], 1)

            for k in "CPVLXH":
                pe.wait_ge(ps_free[k], NB if k == "H" else NT * NB)
            pe.wait_ge(ps_free["M"], (NT - 1) * NB)

            def products(l, b):
                for t in range(NT):
                    n = (l * NB + b) * 4 + t // 2
                    k = (t // 2) % 2
                    if t % 2 == 0 and (b or t >= 4):
                        pe.wait_ge(prod_free, n - 1)
                    last = mm(prod_ps[k][:, (t % 2) * 2 * D:(t % 2 + 1) * 2 * D],
                              rT[:, b, t * P:(t + 1) * P], wscaled[:, 0:2 * D], True, True)
                    if t % 2:
                        last.then_inc(prod_ready, 1)

            def aggregate(l, b):
                pe.wait_ge(low_ready, l * NB + b + 1)
                for k in range(4):
                    n = (l * NB + b) * 4 + k
                    if b or k >= 2:
                        pe.wait_ge(sage_ready, 2 * (n - 1))
                    mm(agg_ps[:, k % 2, 0, 0:1], eye[:, :], ones[:, :], True, True)
                    for h in range(2):
                        t = 2 * k + h
                        for j in range(NT):
                            last = mm(agg_ps[:, k % 2, h, 0:WZ], graph[:, j, b, t * P:(t + 1) * P],
                                      parts[:, b % 2, j, 0:WZ], j == 0, j == NT - 1)
                    last.then_inc(agg_ready, 1)

            def turn(l, b):
                n = l * NB + b
                pe.wait_ge(unit_ready, n + 1)
                if b:
                    pe.wait_ge(moments_ready, 2 * n)
                for t in range(NT):
                    last = pe.transpose(turn_ps[:, t * P:(t + 1) * P], sage[:, b % 2, t, :], eye32[:, :])
                last.then_inc(turn_ready, 1)

            with pe.Fori(0, LAYERS) as l:
                pe.wait_ge(wide_ready, 2 * (l + 1))
                mm(prod_ps[0][:, 0:2 * D], shift_wide[:, 0, :], wcur[:, 0:2 * D], True, True
                   ).then_inc(rowconst_ps, 1)
                pe.wait_ge(prep_step, 2 + 2 * (l + 1))
                products(l, 0)
                products(l, 1)
                for b in range(NB):
                    aggregate(l, b)
                    if b + 2 < NB:
                        products(l, b + 2)
                    if b:
                        turn(l, b - 1)
                turn(l, NB - 1)
                pe.wait_ge(bn_wide, l + 1)
                mm(prod_ps[0][:, 0:D], shift_wide[:, 1, :], wcur[:, 2 * D:3 * D], True, True
                   ).then_inc(head_ps, 1)
                pe.wait_ge(head_w, l + 1)
                for b in range(NB):
                    for h in range(2):
                        n = (l * NB + b) * 2 + h
                        if b == 0:
                            if h == 1:
                                pe.wait_ge(head_const_ready, l + 1)
                        else:
                            pe.wait_ge(y_added, n - 1)
                        for t in range(4):
                            last = mm(prod_ps[(b * 2 + h + 1) % 2][:, t * D:(t + 1) * D],
                                      rT[:, b, (4 * h + t) * P:(4 * h + t + 1) * P],
                                      wscaled[:, 2 * D:3 * D], True, True)
                        last.then_inc(y_ps, 1)


_INS = ["x", "adj", "nodemask"]
_OUT = (NB, N, D)


def kernel(**inputs):
    import numpy as np
    import concourse.bacc as bacc
    from concourse.bass_utils import run_bass_kernel_spmd as run

    nc = bacc.Bacc("TRN2", target_bir_lowering=False, num_devices=1)
    arrays, aps = {}, {}
    for name, value in inputs.items():
        a = np.ascontiguousarray(value)
        arrays[f"in_{name}"] = a
        aps[name] = nc.dram_tensor(f"in_{name}", a.shape, mybir.dt.from_np(a.dtype), kind="ExternalInput").ap()
    result = nc.dram_tensor("result", _OUT, F32, kind="ExternalOutput").ap()

    def each(stem):
        return [aps[f"L0_gnn_{stem}{l}"] for l in (1, 2, 3)]

    build(nc, aps["x"], aps["adj"], aps["nodemask"], each("Wr"), each("Wx"), each("b"), each("g"),
          each("be"), aps["L0_gnn_Wl"], aps["L0_gnn_bl"], result)
    return run(nc, [arrays], core_ids=[0]).results[0]["result"]
```

```python
from contextlib import ExitStack

import concourse.bass as bass
from concourse import mybir

F32, BF16, F16 = mybir.dt.float32, mybir.dt.bfloat16, mybir.dt.float16
F8, I32 = mybir.dt.float8e4, mybir.dt.int32
ALU, ACT, AX = mybir.AluOpType, mybir.ActivationFunctionType, mybir.AxisListType

P = 128
NB, N, D = 8, 1024, 128
NT = N // P
LAYERS = 3
BANK = 512

EDGE = 2048.0
SHIFT = 1024.0
NEVER = 4096.0
FAR = 9000.0
ALL = 1000.0
ROUND = 1.5 * 2.0 ** 23
SWEEPS = [3, 6, 6, 5, 4, 4, 5, 6]
STEPS = 9
SETUP = 11
CODES = 11
GAP, FEW, HALF, SOME, CODE, PARITY, SMALL, HIT, EVEN = range(1, STEPS + 1)

AHEAD = 3
BESIDE_SWEEP, BESIDE_TEST = 1.9, 2.5
FIRST_LOWER = 10
EARLY = 4
RING = 3
WZ = 2 * P + 1
TOP = 2.0 ** 14
ZROW = WZ + 1
BN_EPS, LN_EPS, NORM_EPS = 1e-5, 1e-5, 1e-12


def pieces(lo, hi):
    cuts = [lo] + [c for c in range(BANK, N, BANK) if lo < c < hi] + [hi]
    return list(zip(cuts[:-1], cuts[1:]))


def lower_tasks(i):
    return [task for b in range(NB + 3)
            for task in (("V", i, b), ("K", i, b - 1), ("L", i, b - 2), ("M", i, b - 3)) if 0 <= task[2] < NB]


def order():
    tasks = [("H", 0, b) for b in range(EARLY)] + [("C", 0, b) for b in range(NB)]
    for i in range(NT):
        lower = lower_tasks(i - 1) if i else []
        upper = [("C", i + 1, b) for b in range(NB)] if i + 1 < NT else []
        if i == 0:
            upper = [task for b in range(NB) for task in (("H", 0, b), upper[b]) if task[0] == "C" or b >= EARLY]
        jobs = lower[:FIRST_LOWER] + upper + lower[FIRST_LOWER:]
        tasks.append(("S", i, 0))
        for k in range(SWEEPS[i]):
            tasks.append(("W", i, k))
            tasks += take(jobs, BESIDE_SWEEP)
        tasks.append(("F", i, 0))
        tasks += take(jobs, BESIDE_TEST)
        tasks.append(("T", i, 0))
        for b in range(NB):
            tasks.append(("P", i, b))
            tasks += take(jobs, work(jobs) / (NB - b))
    return tasks + lower_tasks(NT - 1)


def cost(task):
    kind, i, b = task
    tiles = NT - i if kind == "C" else i + 1
    return {"C": 0.053 * tiles * (tiles + 1) / 2, "V": 0.053 * tiles * (tiles + 1) / 2,
            "K": 0.0, "L": 0.053 * 2 * tiles, "M": 0.053 * (tiles + 1), "H": 1.7}[kind]


def work(jobs):
    return sum(map(cost, jobs))


def take(jobs, most):
    out, total = [], 0.0
    while jobs and total + cost(jobs[0]) / 2 < most:
        total += cost(jobs[0])
        out.append(jobs.pop(0))
    return out


TASKS = order()
USES = [task for task in TASKS if task[0] in "CPVLMH"]
SLOT = {use: n % RING for n, use in enumerate(USES)}
BEFORE = {use: USES[n - RING] if n >= RING else None for n, use in enumerate(USES)}


def count(use):
    kind, i, b = use
    return i * NB + b + 1


def sweep_number(i, k):
    return sum(SWEEPS[:i]) + i + k


def build(nc, x, adj, nodemask, wr, wx, bias, gain, shift, wl, bl, out):
    with ExitStack() as ctx:
        def sb(name, shape, dt):
            return ctx.enter_context(nc.sbuf_tensor(name, shape, dt))

        def pb(name, shape, dt=F32):
            return ctx.enter_context(nc.psum_tensor(name, shape, dt))

        def sem(name):
            return ctx.enter_context(nc.semaphore(name))

        graph = sb("graph", [P, NT, NB, N], F8)
        codes = sb("codes", [P, 2 * NB * N], F16)
        ranks = codes[:, :].rearrange("p (q b m) -> p q b m", q=2, b=NB)
        ysum = codes[:, :].bitcast(F32).rearrange("p (b t d) -> p b t d", b=NB, t=NT)
        rT = sb("rT", [P, NB, N], F32)
        arena = sb("arena", [P, 13 * N], F32)
        taken = [0]

        def cut(words, dt=F32):
            taken[0] += words
            piece = arena[:, taken[0] - words:taken[0]]
            return piece if dt == F32 else piece.bitcast(dt)

        hit_rows = cut(4 * N, BF16).rearrange("p (k q m) -> p k q m", k=4, q=2)
        low_codes = cut(N, F16).rearrange("p (q m) -> p q m", q=2)
        diag_codes = cut(N, F16).rearrange("p (q m b) -> p q m b", q=2, b=NB)
        hit = cut(N // 2, BF16).rearrange("p (m b) -> p m b", b=NB)
        last_edge = cut(N // 2, BF16).rearrange("p (m b) -> p m b", b=NB)
        diag_low = cut(N, BF16).rearrange("p (q b c) -> p q b c", q=2, b=NB)
        diag_up = cut(N, BF16).rearrange("p (q b c) -> p q b c", q=2, b=NB)
        taken[0] = 0
        zo = cut(4 * N).rearrange("p (q t c) -> p q t c", q=2, t=NT)
        parts = cut(NT * ZROW, F16).rearrange("p (q t c) -> p q t c", q=2, t=NT)
        sage = cut(2 * N).rearrange("p (q t d) -> p q t d", q=2, t=NT)
        squares = cut(N // 2, BF16)
        part_sum = cut(4 * D).rearrange("p (q t d) -> p q t d", q=2, t=2)
        shift_wide = cut(P)
        rowconst = cut(2 * D)
        wcur = cut(3 * D)
        wscaled = cut(3 * D)
        xin = sb("xin", [P, 2, NT, D], F32)
        x_again = ([xin[:, b, :, :] for b in range(2)]
                   + [arena[:, b * N:(b + 1) * N].rearrange("p (t d) -> p t d", t=NT) for b in range(4)]
                   + [sage[:, b, :, :] for b in range(2)])
        stair = sb("stair", [P, N], BF16)
        eye = sb("eye", [P, P], BF16)
        neg_eye = sb("neg_eye", [P, P], BF16)
        off_eye = sb("off_eye", [P, P], F16)
        low_mask = sb("low_mask", [P, P], F32)
        up_mask = sb("up_mask", [P, P], F32)
        eye32 = sb("eye32", [P, P], F32)
        ones = sb("ones", [P, 1], BF16)
        zeros = sb("zeros", [P, NB], BF16)
        mask_rows = sb("mask_rows", [NB * NT, P], I32)
        vectors = sb("vectors", [NB * NT + 2 * LAYERS, P], F32)
        columns = sb("columns", [P, NB * NT + 2 * LAYERS], F32)
        mask = columns[:, 0:NB * NT].rearrange("p (b t) -> p b t", b=NB)
        live = sb("live", [P, NB, NT], F32)
        left_right = sb("left_right", [P, 2, NB], F32)
        gap0, few_at, some_at, last_at = (sb(n, [P, NB], F32) for n in
                                          ("gap0", "few_at", "some_at", "last_at"))
        last_code = sb("last_code", [P, NB], F16)
        gap = sb("gap", [P, 2, NB], F32)
        few, half, some, parity = (sb(n, [P, NB], F32) for n in ("few", "half", "some", "parity"))
        code = sb("code", [P, NB], F16)
        small, even, changed = (sb(n, [P, NB], BF16) for n in ("small", "even", "changed"))
        flag = sb("flag", [1, 1], I32)
        edge_a, edge_b, left = (sb(n, [P, NB], F32) for n in ("edge_a", "edge_b", "left"))
        left_low = sb("left_low", [P, NB], F32)
        rule = sb("rule", [P, 5, 2, NB], F32)
        mid_a, mid_b, mid_c = (sb(n, [P, NB], F32) for n in ("mid_a", "mid_b", "mid_c"))
        ln_stats, ln_mv = sb("ln_stats", [P, NT, 6], F32), sb("ln_mv", [P, 2, NT, 2], F32)
        ln_std, ln_inv = sb("ln_std", [P, 2, NT], F32), sb("ln_inv", [P, NT], F32)
        zback = sb("zback", [P, 1], F32)
        wabs = sb("wabs", [P, D], F32)
        reach = sb("reach", [P, 3, LAYERS], F32)
        reach_wide = sb("reach_wide", [P, P], F32)
        zscale = sb("zscale", [P, 2, LAYERS], F32)
        wraw = sb("wraw", [P, LAYERS, 3 * D], F32)
        bias_wide = sb("bias_wide", [P, LAYERS, 2 * D], F32)
        head_const = sb("head_const", [P, D], F32)
        degree = sb("degree", [P, 2, 2], F32)
        norms = sb("norms", [P, 4, NT], F32)
        moments = sb("moments", [P, 2, NB], F32)
        bn = sb("bn", [P, 10], F32)
        affine = sb("affine", [P, 2], F32)

        ring = pb("ring", [P, RING, 2 * BANK])
        counts = pb("counts", [P, BANK])
        spare = pb("spare", [P, BANK])
        removed = counts[:, 0:NB]
        agg_ps = ring[:, 0:2, :].rearrange("p s (k c) -> p s k c", k=2)
        turn_ps = ring[:, 2, :]
        prod_ps = [counts, spare]

        adj_in = [sem(f"adj_in{i}") for i in range(NT)]
        x_in = [sem(f"x_in{b}") for b in range(NB)]
        params_in, mask_in, weights_in = sem("params_in"), sem("mask_in"), sem("weights_in")
        consts_made, rows_ready = sem("consts_made"), sem("rows_ready")
        pool_step, triangles_ready, diag_codes_ready = sem("pool_step"), sem("triangles_ready"), sem("diag_codes_ready")
        columns_ps, columns_ready = sem("columns_ps"), sem("columns_ready")
        ps_ready = {k: sem(f"ps_ready_{k}") for k in "CPVLMH"}
        ps_free = {k: sem(f"ps_free_{k}") for k in "CPVLMH"}
        removed_ready = sem("removed_ready")
        setup_step, sweep_step = sem("setup_step"), sem("sweep_step")
        final_step, changed_ready, flag_ps, flag_ready = (
            sem(n) for n in ("final_step", "changed_ready", "flag_ps", "flag_ready"))
        more_step = [sem(f"more_step{i}") for i in range(NT)]
        more_removed = [sem(f"more_removed{i}") for i in range(NT)]
        hits_up, hits_low = sem("hits_up"), sem("hits_low")
        ln_stat, ln_var, ln_root, ln_scale, ln_done = (
            sem(n) for n in ("ln_stat", "ln_var", "ln_root", "ln_scale", "ln_done"))
        reach_step, reach_made, reach_ps = sem("reach_step"), sem("reach_made"), sem("reach_ps")
        prep_step, wide_ready, rowconst_ps = sem("prep_step"), sem("wide_ready"), sem("rowconst_ps")
        prod_ready, prod_free = sem("prod_ready"), sem("prod_free")
        top_ready, low_ready = sem("top_ready"), sem("low_ready")
        agg_ready, sage_step, sage_ready = sem("agg_ready"), sem("sage_step"), sem("sage_ready")
        squared, root_ready, norm_step, unit_ready = (
            sem(n) for n in ("squared", "root_ready", "norm_step", "unit_ready"))
        turn_ready, turned, moments_ready = sem("turn_ready"), sem("turned"), sem("moments_ready")
        bn_step, bn_var, bn_root, head_step = (sem(n) for n in ("bn_step", "bn_var", "bn_root", "head_step"))
        y_ps, y_added = sem("y_ps"), sem("y_added")
        last_step, again_in, stored = (
            sem("last_step"), [sem(f"again_in{b}") for b in range(NB)], sem("stored"))
        ysum_cleared, scaled = sem("ysum_cleared"), sem("scaled")
        out_ready = sem("out_ready")

        def slot(use):
            return ring[:, SLOT[use], :]

        def hits(kind, b):
            return [hit_rows[:, k, b % 2, :] for k in ((0, 1) if kind == "U" else (2,))]

        block = ctx.enter_context(nc.Block())

        @block.sync
        def _(sp):
            sp.dma_start(mask_rows[:, :], nodemask.rearrange("b (t p) -> (b t) p", p=P)).then_inc(mask_in, 16)
            for l in range(LAYERS):
                r = NB * NT + l
                sp.dma_start(vectors[r:r + 1, :], gain[l].unsqueeze(0)).then_inc(params_in, 16)
                sp.dma_start(vectors[r + LAYERS:r + LAYERS + 1, :], shift[l].unsqueeze(0)).then_inc(params_in, 16)
            for b in range(NB):
                sp.dma_start(rT[:, b, :].rearrange("p (t d) -> p t d", t=NT),
                             x[b].rearrange("(t p) d -> p t d", p=P)).then_inc(x_in[b], 16)
            for l in range(LAYERS):
                for k, w in enumerate((wr, wx, wl)):
                    src = w[l] if k < 2 else wl[l * D:(l + 1) * D, :]
                    sp.dma_start(wraw[:, l, k * D:(k + 1) * D], src).then_inc(weights_in, 16)
                sp.dma_start(bias_wide[:, l, D:2 * D], bias[l].unsqueeze(0).broadcast_to([P, D])
                             ).then_inc(weights_in, 16)
            sp.dma_start(head_const[:, :], bl.unsqueeze(0).broadcast_to([P, D])).then_inc(weights_in, 16)
            for b in range(NB):
                if b == 2:
                    sp.wait_ge(sage_ready, LAYERS * NB * NT)
                    sp.wait_ge(low_ready, LAYERS * NB)
                elif b == 6:
                    sp.wait_ge(turn_ready, LAYERS * NB)
                sp.dma_start(x_again[b], x[b].rearrange("(t p) d -> p t d", p=P)).then_inc(again_in[b], 16)
            for b in range(NB):
                sp.wait_ge(out_ready, b + 1)
                sp.dma_start(out[b].rearrange("(t p) d -> p t d", p=P), x_again[b]).then_inc(stored, 16)
            sp.wait_ge(stored, 16 * NB)

        @block.gpsimd
        def _(pool):
            made = 0
            for tile, value in ((eye[:, :], 0.0), (neg_eye[:, :], 0.0), (eye32[:, :], 0.0),
                                (off_eye[:, :], 1.0), (stair[:, :], 1.0), (low_mask[:, :], 1.0),
                                (up_mask[:, :], 1.0), (ones[:, :], 1.0), (zeros[:, :], 0.0),
                                (bias_wide[:, :, 0:D], 0.0)):
                made += 1
                pool.memset(tile, value).then_inc(pool_step, 1)
            pool.wait_ge(pool_step, made)

            def select(tile, op, fill, sign):
                return pool.affine_select(out=tile, in_=tile, compare_op=op, fill=fill, base=0,
                                          pattern=[[sign, P]], channel_multiplier=-sign)

            select(eye[:, :], ALU.not_equal, 1.0, 1).then_inc(consts_made, 1)
            select(neg_eye[:, :], ALU.not_equal, -1.0, 1).then_inc(consts_made, 1)
            select(eye32[:, :], ALU.not_equal, 1.0, 1).then_inc(consts_made, 1)
            select(off_eye[:, :], ALU.not_equal, 0.0, 1).then_inc(consts_made, 1)
            select(low_mask[:, :], ALU.is_ge, 0.0, -1).then_inc(consts_made, 1)
            select(up_mask[:, :], ALU.is_gt, 0.0, 1).then_inc(consts_made, 1)
            select(stair[:, 0:P], ALU.is_ge, 0.0, 1).then_inc(pool_step, 1)
            pool.wait_ge(pool_step, made + 1)
            select(stair[:, 0:P], ALU.not_equal, EDGE, 1).then_inc(consts_made, 1)
            pool.wait_ge(consts_made, 7)
            step = made + 1

            def load(i, b):
                tiles = adj[b, i * P:N, i * P:(i + 1) * P].rearrange("(j p) c -> p j c", p=P)
                pool.dma_start(graph[:, i:NT, b, i * P:(i + 1) * P], tiles).then_inc(adj_in[i], 16)

            def triangles(i):
                pool.wait_ge(adj_in[i], 16 * NB)
                if i >= 2:
                    pool.wait_ge(ps_ready["P"], (i - 1) * NB)
                diag = graph[:, i, :, i * P:(i + 1) * P]
                for tile, mask_ in ((diag_low, low_mask), (diag_up, up_mask)):
                    pool.tensor_tensor(tile[:, i % 2, :, :], diag,
                                       mask_[:, :].unsqueeze(1).broadcast_to([P, NB, P]),
                                       ALU.mult).then_inc(triangles_ready, 1)

            for i in range(AHEAD):
                for b in range(NB):
                    load(i, b)
                if i < 2:
                    triangles(i)
            for kind, i, b in TASKS:
                if kind == "C" and b == NB - 1:
                    pool.wait_ge(ps_free["C"], (i + 1) * NB)
                    d = ranks[:, i % 2, :, 0:P]
                    pool.tensor_tensor(d, d, off_eye[:, :].unsqueeze(1).broadcast_to([P, NB, P]),
                                       ALU.mult).then_inc(pool_step, 1)
                    step += 1
                    pool.wait_ge(pool_step, step)
                    if i >= 2:
                        pool.wait_ge(final_step, (i - 1) * CODES)
                    pool.tensor_copy(diag_codes[:, i % 2, :, :].rearrange("p m b -> p b m"), d
                                     ).then_inc(diag_codes_ready, 1)
                elif kind == "P":
                    if i + AHEAD < NT:
                        load(i + AHEAD, b)
                    if b == NB - 1 and i + 2 < NT:
                        triangles(i + 2)
            for k in "CPVLMH":
                pool.wait_ge(ps_free[k], NB if k == "H" else NT * NB)
            pool.memset(parts[:, :, :, 2 * D:WZ], 1.0).then_inc(pool_step, 1)
            pool.wait_ge(pool_step, step + 1)

            def low(l, b):
                pool.wait_ge(top_ready, l * NB + b + 1)
                pool.tensor_tensor(parts[:, b % 2, :, D:2 * D], zo[:, b % 2, :, 0:D],
                                   parts[:, b % 2, :, 0:D], ALU.subtract).then_inc(low_ready, 1)

            for b in range(NB):
                low(0, b)
                if b == 1:
                    pool.wait_ge(hits_up, 2 * NT * NB)
                    pool.memset(ysum[:, :, :, :].rearrange("p b t d -> p (b t d)"), 0.0).then_inc(ysum_cleared, 1)
            with pool.Fori(1, LAYERS) as l:
                for b in range(NB):
                    low(l, b)
            for b in range(NB):
                pool.wait_ge(again_in[b], 16)
                pool.wait_ge(scaled, (b + 1) * NT)
                pool.tensor_tensor(x_again[b], x_again[b], ysum[:, b, :, :], ALU.add).then_inc(out_ready, 1)

        @block.vector
        def _(dve):
            dve.wait_ge(mask_in, 16)
            dve.tensor_copy(vectors[0:NB * NT, :], mask_rows[:, :]).then_inc(rows_ready, 1)
            dve.wait_ge(columns_ps, 1)
            dve.tensor_copy(columns[:, :], spare[:, 0:NB * NT + 2 * LAYERS]).then_inc(columns_ready, 1)
            dve.wait_ge(columns_ready, 1)
            dve.tensor_scalar(live[:, :, :], mask, 0.0, None, ALU.not_equal).then_inc(columns_ready, 1)
            dve.wait_ge(columns_ready, 2)

            def setup(i):
                n = i * SETUP
                dve.wait_ge(removed_ready, sweep_number(i, 0) + 1)
                dve.tensor_copy(left_right[:, :, :], counts[:, NB:3 * NB].rearrange("p (k b) -> p k b", k=2)
                                ).then_inc(setup_step, 1)
                dve.wait_ge(setup_step, n + 1)
                l0, u = left_right[:, 0, :], left_right[:, 1, :]
                alive = live[:, :, i]
                dve.tensor_tensor(gap0[:, :], u, l0, ALU.subtract).then_inc(setup_step, 1)
                dve.scalar_tensor_tensor(few_at[:, :], u, FAR - 5.0, alive, ALU.add, ALU.mult).then_inc(setup_step, 1)
                dve.scalar_tensor_tensor(some_at[:, :], u, FAR - 0.5, alive, ALU.add, ALU.mult).then_inc(setup_step, 1)
                dve.tensor_scalar(last_at[:, :], u, -1.0, FAR - SHIFT + 1.0, ALU.mult, ALU.add).then_inc(setup_step, 1)
                dve.tensor_scalar(last_code[:, :], u, SHIFT - 1.0, None, ALU.add).then_inc(setup_step, 1)
                dve.tensor_scalar(left_low[:, :], l0, EDGE - SHIFT, None, ALU.add).then_inc(setup_step, 1)
                dve.wait_ge(setup_step, n + 7)
                dve.tensor_scalar(gap0[:, :], gap0[:, :], 0.5, 0.25, ALU.mult, ALU.add).then_inc(setup_step, 1)
                dve.tensor_scalar(few_at[:, :], few_at[:, :], -FAR, None, ALU.add).then_inc(setup_step, 1)
                dve.tensor_scalar(some_at[:, :], some_at[:, :], -FAR, None, ALU.add).then_inc(setup_step, 1)
                dve.wait_ge(diag_codes_ready, i + 1)
                dve.tensor_tensor(last_edge[:, :, :], diag_codes[:, i % 2, :, :],
                                  last_code[:, :].unsqueeze(1).broadcast_to([P, P, NB]),
                                  ALU.is_equal).then_inc(setup_step, 1)
                dve.wait_ge(setup_step, n + SETUP)

            def sweep(i, gap_now, done, at, with_hits):
                dve.scalar_tensor_tensor(gap_now, removed, 0.5, gap0[:, :], ALU.mult, ALU.add).then_inc(done, 1)
                dve.wait_ge(done, at + GAP)
                dve.tensor_tensor(few[:, :], gap_now, few_at[:, :], ALU.is_ge).then_inc(done, 1)
                dve.tensor_scalar(half[:, :], gap_now, ROUND, ROUND - SHIFT + 1.0, ALU.add,
                                  ALU.subtract).then_inc(done, 1)
                dve.tensor_tensor(some[:, :], gap_now, some_at[:, :], ALU.is_lt).then_inc(done, 1)
                dve.wait_ge(done, at + HALF)
                dve.scalar_tensor_tensor(code[:, :], few[:, :], NEVER, half[:, :], ALU.mult,
                                         ALU.max).then_inc(done, 1)
                dve.tensor_tensor(parity[:, :], gap_now, half[:, :], ALU.subtract).then_inc(done, 1)
                dve.wait_ge(done, at + SOME)
                dve.tensor_tensor(small[:, :], few[:, :], some[:, :], ALU.mult).then_inc(done, 1)
                dve.wait_ge(done, at + CODE)
                if with_hits:
                    dve.tensor_tensor(hit[:, :, :], diag_codes[:, i % 2, :, :],
                                      code[:, :].unsqueeze(1).broadcast_to([P, P, NB]),
                                      ALU.is_equal).then_inc(done, 1)
                else:
                    dve.tensor_tensor(changed[:, :], gap[:, 0, :], gap[:, 1, :], ALU.not_equal).then_inc(done, 1)
                dve.wait_ge(done, at + PARITY)
                dve.scalar_tensor_tensor(even[:, :], parity[:, :], 1.0 - SHIFT, few[:, :], ALU.is_gt,
                                         ALU.is_gt).then_inc(done, 1)

            def codes_of(i, done, at):
                up_code, up_from, low_bias, low_code, low_scale = (rule[:, k, i % 2, :] for k in range(5))
                dve.tensor_tensor(edge_a[:, :], even[:, :], last_at[:, :], ALU.mult).then_inc(done, 1)
                dve.tensor_tensor(left[:, :], left_low[:, :], removed, ALU.subtract).then_inc(done, 1)
                dve.tensor_tensor(mid_a[:, :], last_code[:, :], code[:, :], ALU.subtract).then_inc(done, 1)
                dve.wait_ge(done, at + 1)
                dve.scalar_tensor_tensor(edge_b[:, :], small[:, :], FAR - ALL, edge_a[:, :], ALU.mult,
                                         ALU.add).then_inc(done, 1)
                dve.wait_ge(done, at + 3)
                dve.scalar_tensor_tensor(mid_b[:, :], mid_a[:, :], 0.5, even[:, :], ALU.mult,
                                         ALU.mult).then_inc(done, 1)
                dve.tensor_tensor(mid_c[:, :], left[:, :], code[:, :], ALU.add).then_inc(done, 1)
                dve.wait_ge(done, at + 4)
                dve.tensor_scalar(up_from, edge_b[:, :], -1.0, FAR, ALU.mult, ALU.add).then_inc(done, 1)
                dve.wait_ge(done, at + 6)
                dve.tensor_tensor(low_code, mid_b[:, :], few[:, :], ALU.subtract).then_inc(done, 1)
                dve.tensor_scalar(low_scale, small[:, :], -1.0, 1.0, ALU.mult, ALU.add).then_inc(done, 1)
                dve.tensor_copy(up_code, code[:, :]).then_inc(done, 1)
                dve.wait_ge(done, at + 8)
                dve.scalar_tensor_tensor(low_bias, mid_c[:, :], -1.0, low_code, ALU.mult,
                                         ALU.subtract).then_inc(done, 1)

            def final(i):
                g = sweep_number(i, SWEEPS[i])
                dve.wait_ge(removed_ready, g + 1)
                dve.wait_ge(sweep_step, STEPS * g)
                sweep(i, gap[:, SWEEPS[i] % 2, :], sweep_step, STEPS * g, False)
                dve.wait_ge(sweep_step, STEPS * (g + 1))
                if i >= 2:
                    dve.wait_ge(ps_free["L"], (i - 1) * NB)
                codes_of(i, final_step, i * CODES)

            def test(i):
                dve.wait_ge(flag_ps, i + 1)
                dve.tensor_reduce(flag[:, :], spare[0:1, 0:NB], AX.X, ALU.max).then_inc(flag_ready, 1)
                dve.wait_ge(flag_ready, i + 1)
                more = dve.value_load(flag[0:1, 0:1], min_val=0, max_val=P)
                dve.wait_ge(final_step, (i + 1) * CODES)
                with dve.If(more > 0):
                    with dve.Fori(0, P) as k:
                        sweep(i, gap[:, 0, :], more_step[i], k * STEPS, True)
                        dve.wait_ge(more_step[i], k * STEPS + EVEN)
                        dve.wait_ge(more_removed[i], k + 1)
                    sweep(i, gap[:, 0, :], more_step[i], P * STEPS, False)
                    dve.wait_ge(more_step[i], (P + 1) * STEPS)
                    codes_of(i, more_step[i], (P + 1) * STEPS)
                    dve.wait_ge(more_step[i], (P + 1) * STEPS + CODES)

            def mark_up(i, b):
                n = i * NB + b
                width = N - i * P
                if n >= 2:
                    dve.wait_ge(ps_ready["P"], n - 1)
                for k, op in ((0, ALU.is_equal), (1, ALU.is_ge)):
                    dve.tensor_scalar(hits("U", b)[k][:, 0:width], ranks[:, i % 2, b, 0:width],
                                      rule[:, k, i % 2, b:b + 1], None, op).then_inc(hits_up, 1)

            def mark_low(i, b):
                n = i * NB + b
                width = (i + 1) * P
                dve.wait_ge(ps_free["V"], n + 1)
                if n >= 2:
                    dve.wait_ge(ps_ready["L"], n - 1)
                dve.tensor_scalar(hits("L", b)[0][:, 0:width], low_codes[:, b % 2, 0:width],
                                  rule[:, 3, i % 2, b:b + 1], None, ALU.is_equal).then_inc(hits_low, 1)

            def norm_input(b):
                xb = rT[:, b, :].rearrange("p (t d) -> p t d", t=NT)
                dve.wait_ge(x_in[b], 16)
                for t in range(NT):
                    dve.bn_stats(ln_stats[:, t, :], xb[:, t, :]).then_inc(ln_stat, 1)
                n = 2 * NT * b
                for t in range(NT):
                    dve.wait_ge(ln_stat, n + NT)
                    dve.bn_aggr(ln_mv[:, b % 2, t, :], ln_stats[:, t, :]).then_inc(ln_stat, 1)
                dve.wait_ge(ln_stat, n + 2 * NT)
                dve.tensor_scalar(ln_std[:, 0, :], ln_mv[:, b % 2, :, 1], LN_EPS, None, ALU.add).then_inc(ln_var, 1)
                dve.wait_ge(ln_root, b + 1)
                dve.reciprocal(ln_inv[:, :], ln_std[:, 1, :]).then_inc(ln_scale, 1)
                dve.wait_ge(ln_scale, b + 1)
                for t in range(NT):
                    dve.tensor_scalar(xb[:, t, :], xb[:, t, :], ln_mv[:, b % 2, t, 0:1], ln_inv[:, t:t + 1],
                                      ALU.subtract, ALU.mult).then_inc(ln_done, 1)
                dve.wait_ge(ln_done, (b + 1) * NT)

            for kind, i, b in TASKS:
                if kind == "S":
                    setup(i)
                elif kind == "W":
                    g = sweep_number(i, b)
                    dve.wait_ge(removed_ready, g + 1)
                    if g:
                        dve.wait_ge(sweep_step, STEPS * g)
                    sweep(i, gap[:, b % 2, :], sweep_step, STEPS * g, True)
                elif kind == "F":
                    final(i)
                elif kind == "T":
                    test(i)
                elif kind == "P":
                    mark_up(i, b)
                elif kind == "K":
                    mark_low(i, b)
                elif kind == "H":
                    norm_input(b)

            dve.wait_ge(weights_in, 16 * (4 * LAYERS + 1))
            made = 0
            dve.memset(reach[:, 0, 0:1], float(D) ** 0.5).then_inc(reach_step, 1)
            gains = columns[:, NB * NT:NB * NT + LAYERS - 1]
            shifts = columns[:, NB * NT + LAYERS:NB * NT + 2 * LAYERS - 1]
            dve.tensor_scalar(reach[:, 1, 0:2], gains, -1.0, None, ALU.mult).then_inc(reach_step, 1)
            dve.tensor_scalar(reach[:, 2, 0:2], shifts, -1.0, None, ALU.mult).then_inc(reach_step, 1)
            dve.wait_ge(reach_step, 3)
            dve.tensor_tensor(reach[:, 1, 0:2], reach[:, 1, 0:2], gains, ALU.max).then_inc(reach_step, 1)
            dve.tensor_tensor(reach[:, 2, 0:2], reach[:, 2, 0:2], shifts, ALU.max).then_inc(reach_step, 1)
            dve.wait_ge(reach_step, 5)
            dve.scalar_tensor_tensor(reach[:, 0, 1:3], reach[:, 1, 0:2], float(NB * N) ** 0.5 * 1.01,
                                     reach[:, 2, 0:2], ALU.mult, ALU.add).then_inc(reach_step, 1)
            dve.wait_ge(reach_step, 6)
            for l in range(LAYERS):
                if l:
                    dve.wait_ge(reach_ps, l)
                dve.tensor_scalar(wabs[:, :], wraw[:, l, 0:D], -1.0, None, ALU.mult).then_inc(reach_made, 1)
                dve.tensor_copy(reach_wide[:, :], reach[:, 0, l:l + 1].broadcast_to([P, P])).then_inc(reach_made, 1)
                dve.wait_ge(reach_made, 3 * l + 2)
                dve.tensor_tensor(wabs[:, :], wabs[:, :], wraw[:, l, 0:D], ALU.max).then_inc(reach_made, 1)
                dve.wait_ge(reach_ps, l + 1)
                n = 6 + 5 * l
                up, back = zscale[:, 0, l:l + 1], zscale[:, 1, l:l + 1]
                dve.tensor_reduce(back, spare[:, D:2 * D], AX.X, ALU.max).then_inc(reach_step, 1)
                dve.wait_ge(reach_step, n + 1)
                dve.tensor_scalar(back, back, 1e-30, None, ALU.max).then_inc(reach_step, 1)
                dve.wait_ge(reach_step, n + 2)
                dve.tensor_scalar(back.bitcast(I32), back.bitcast(I32), 0x7F800000, None,
                                  ALU.bitwise_and).then_inc(reach_step, 1)
                dve.wait_ge(reach_step, n + 3)
                dve.tensor_scalar(back, back, 1.0 / TOP, None, ALU.mult).then_inc(reach_step, 1)
                dve.wait_ge(reach_step, n + 4)
                dve.reciprocal(up, back).then_inc(reach_step, 1)
                dve.wait_ge(reach_step, n + 5)

            for k in "CPVLMH":
                dve.wait_ge(ps_free[k], NB if k == "H" else NT * NB)
            dve.memset(affine[:, 0:1], 1.0).then_inc(prep_step, 1)
            dve.memset(affine[:, 1:2], 0.0).then_inc(prep_step, 1)
            dve.wait_ge(prep_step, 2)

            def products(l, b):
                for k in range(NT // 2):
                    n = (l * NB + b) * 4 + k
                    dve.wait_ge(prod_ready, n + 1)
                    dve.tensor_tensor(zo[:, b % 2, 2 * k:2 * k + 2, :],
                                      prod_ps[k % 2][:, :].rearrange("p (t c) -> p t c", t=2),
                                      rowconst[:, :].unsqueeze(1).broadcast_to([P, 2, 2 * D]),
                                      ALU.add).then_inc(prod_free, 1)

            def combine(l, b):
                for k in range(4):
                    n = (l * NB + b) * 4 + k
                    dve.wait_ge(agg_ready, n + 1)
                    ps = agg_ps[:, k % 2, :, :]
                    dve.tensor_scalar(degree[:, 0, :], ps[:, :, 2 * D], 1.0, None, ALU.max).then_inc(sage_step, 1)
                    dve.tensor_reduce(part_sum[:, k % 2, :, :], ps[:, :, 0:2 * D].rearrange(
                        "p t (s d) -> p t d s", s=2), AX.X, ALU.add).then_inc(sage_step, 1)
                    dve.wait_ge(sage_step, 4 * n + 1)
                    dve.reciprocal(degree[:, 1, :], degree[:, 0, :]).then_inc(sage_step, 1)
                    dve.wait_ge(sage_step, 4 * n + 3)
                    dve.tensor_scalar(degree[:, 1, :], degree[:, 1, :], zback[:, :], None, ALU.mult
                                      ).then_inc(sage_step, 1)
                    dve.wait_ge(sage_step, 4 * n + 4)
                    for h in range(2):
                        t = 2 * k + h
                        dve.scalar_tensor_tensor(sage[:, b % 2, t, :], part_sum[:, k % 2, h, :],
                                                 degree[:, 1, h:h + 1], zo[:, b % 2, t, D:2 * D],
                                                 ALU.mult, ALU.add).then_inc(sage_ready, 1)
                    dve.wait_ge(sage_ready, 2 * (n + 1))

            def unit(l, b):
                n = l * NB + b
                dve.wait_ge(root_ready, n + 1)
                dve.tensor_scalar(norms[:, 2, :], norms[:, 1, :], NORM_EPS, None, ALU.max).then_inc(norm_step, 1)
                dve.wait_ge(norm_step, 3 * n + 1)
                dve.reciprocal(norms[:, 3, :], norms[:, 2, :]).then_inc(norm_step, 1)
                dve.wait_ge(norm_step, 3 * n + 2)
                dve.tensor_tensor(norms[:, 3, :], norms[:, 3, :], mask[:, b, :], ALU.mult).then_inc(norm_step, 1)
                dve.wait_ge(norm_step, 3 * n + 3)
                dve.tensor_tensor(sage[:, b % 2, :, :], sage[:, b % 2, :, :],
                                  norms[:, 3, :].unsqueeze(2).broadcast_to([P, NT, D]),
                                  ALU.mult).then_inc(unit_ready, 1)
                dve.wait_ge(unit_ready, n + 1)

            def batch_norm(l):
                c = l * BN
                dve.wait_ge(moments_ready, 2 * NB * (l + 1))
                dve.tensor_reduce(bn[:, 0:2], moments[:, :, :], AX.X, ALU.add).then_inc(bn_step, 1)
                dve.wait_ge(bn_step, c + 1)
                dve.tensor_scalar(bn[:, 2:4], bn[:, 0:2], 1.0 / (NB * N), None, ALU.mult).then_inc(bn_step, 1)
                dve.wait_ge(bn_step, c + 2)
                dve.tensor_tensor(bn[:, 4:5], bn[:, 2:3], bn[:, 2:3], ALU.mult).then_inc(bn_step, 1)
                dve.wait_ge(bn_step, c + 3)
                dve.tensor_tensor(bn[:, 5:6], bn[:, 3:4], bn[:, 4:5], ALU.subtract).then_inc(bn_step, 1)
                dve.wait_ge(bn_step, c + 4)
                dve.tensor_scalar(bn[:, 6:7], bn[:, 5:6], 0.0, BN_EPS, ALU.max, ALU.add).then_inc(bn_var, 1)
                dve.wait_ge(bn_root, l + 1)
                dve.reciprocal(bn[:, 8:9], bn[:, 7:8]).then_inc(bn_step, 1)
                dve.wait_ge(bn_step, c + 5)
                gcol = columns[:, bass.ds(l + NB * NT, 1)]
                bcol = columns[:, bass.ds(l + NB * NT + LAYERS, 1)]
                dve.tensor_tensor(affine[:, 0:1], gcol, bn[:, 8:9], ALU.mult).then_inc(bn_step, 1)
                dve.wait_ge(bn_step, c + 6)
                dve.tensor_tensor(bn[:, 4:5], bn[:, 2:3], affine[:, 0:1], ALU.mult).then_inc(bn_step, 1)
                dve.wait_ge(bn_step, c + 7)
                dve.tensor_tensor(affine[:, 1:2], bcol, bn[:, 4:5], ALU.subtract).then_inc(bn_step, 1)
                dve.wait_ge(bn_step, c + 8)

            def head_weights(l):
                lw = wraw[:, bass.ds(l, 1), :].rearrange("p a c -> p (a c)")
                dve.tensor_copy(wcur[:, 2 * D:3 * D], lw[:, 2 * D:3 * D]).then_inc(head_step, 1)
                dve.wait_ge(head_step, 2 * l + 1)

            def head_constant(l):
                dve.tensor_tensor(head_const[:, :], head_const[:, :], prod_ps[0][:, 2 * D:3 * D], ALU.add
                                  ).then_inc(head_step, 1)

            def head_rows(l, b):
                for h in range(2):
                    dve.wait_ge(y_ps, (l * NB + b) * 2 + h + 1)
                    dve.tensor_tensor(ysum[:, b, 4 * h:4 * h + 4, :], ysum[:, b, 4 * h:4 * h + 4, :],
                                      prod_ps[h][:, :].rearrange("p (t d) -> p t d", t=4),
                                      ALU.add).then_inc(y_added, 1)

            def layer(l, first):
                at = 2 + l * PREP
                lw = wraw[:, bass.ds(l, 1), :].rearrange("p a c -> p (a c)")
                dve.tensor_scalar(wcur[:, 0:D], lw[:, 0:D], zscale[:, 0, bass.ds(l, 1)], None, ALU.mult
                                  ).then_inc(prep_step, 1)
                dve.tensor_copy(zback[:, :], zscale[:, 1, bass.ds(l, 1)]).then_inc(prep_step, 1)
                dve.tensor_copy(wcur[:, D:2 * D], lw[:, D:2 * D]).then_inc(prep_step, 1)
                if not first:
                    head_weights(l - 1)
                    batch_norm(l - 1)
                width = 2 * D if first else 3 * D
                dve.tensor_copy(shift_wide[:, :], affine[:, 1:2].broadcast_to([P, P])).then_inc(wide_ready, 1)
                dve.wait_ge(prep_step, at + 3)
                dve.tensor_scalar(wscaled[:, 0:width], wcur[:, 0:width], affine[:, 0:1], None, ALU.mult
                                  ).then_inc(wide_ready, 1)
                dve.wait_ge(rowconst_ps, l + 1)
                bw = bias_wide[:, bass.ds(l, 1), :].rearrange("p a c -> p (a c)")
                dve.tensor_tensor(rowconst[:, :], prod_ps[0][:, 0:2 * D], bw, ALU.add).then_inc(prep_step, 1)
                if not first:
                    head_constant(l - 1)
                dve.wait_ge(prep_step, at + PREP)
                products(l, 0)
                products(l, 1)
                for b in range(NB):
                    combine(l, b)
                    if b + 2 < NB:
                        products(l, b + 2)
                    if b and not first:
                        head_rows(l - 1, b - 1)
                    unit(l, b)
                if not first:
                    head_rows(l - 1, NB - 1)
                    dve.wait_ge(y_added, l * 2 * NB)

            PREP, BN = 4, 8
            layer(0, True)
            dve.wait_ge(ysum_cleared, 1)
            with dve.Fori(1, LAYERS) as l:
                layer(l, False)
            l = LAYERS - 1
            head_weights(l)
            batch_norm(l)
            dve.tensor_copy(shift_wide[:, :], affine[:, 1:2].broadcast_to([P, P])).then_inc(wide_ready, 1)
            dve.tensor_scalar(wscaled[:, 2 * D:3 * D], wcur[:, 2 * D:3 * D], affine[:, 0:1], None, ALU.mult
                              ).then_inc(wide_ready, 1)
            dve.wait_ge(rowconst_ps, LAYERS + 1)
            dve.wait_ge(head_step, 2 * l + 1)
            head_constant(l)
            dve.wait_ge(head_step, 2 * LAYERS)
            for b in range(NB):
                head_rows(l, b)
                dve.wait_ge(y_added, (l * NB + b + 1) * 2)
                dve.tensor_tensor(ysum[:, b, :, :], ysum[:, b, :, :],
                                  head_const[:, :].unsqueeze(1).broadcast_to([P, NT, D]), ALU.add
                                  ).then_inc(last_step, 1)

        @block.scalar
        def _(act):
            for kind, i, b in TASKS:
                if kind == "C":
                    use = ("C", i, b)
                    act.wait_ge(ps_ready["C"], count(use))
                    if i >= 2:
                        act.wait_ge(hits_up, 2 * ((i - 2) * NB + b + 1))
                    act.activation(ranks[:, i % 2, b, 0:N - i * P], slot(use)[:, 0:N - i * P], ACT.Copy,
                                   bias=-SHIFT).then_inc(ps_free["C"], 1)
                elif kind == "P":
                    use = ("P", i, b)
                    act.wait_ge(ps_ready["P"], count(use))
                    act.activation(graph[:, i, b, i * P:N], slot(use)[:, 0:N - i * P], ACT.Copy,
                                   saturate=False).then_inc(ps_free["P"], 1)
                elif kind == "V":
                    use = ("V", i, b)
                    act.wait_ge(ps_ready["V"], count(use))
                    n = count(use)
                    if n > 2:
                        act.wait_ge(hits_low, n - 2)
                    act.activation(low_codes[:, b % 2, 0:(i + 1) * P], slot(use)[:, 0:(i + 1) * P], ACT.Abs,
                                   bias=rule[:, 2, i % 2, b:b + 1]).then_inc(ps_free["V"], 1)
                elif kind == "L":
                    use = ("L", i, b)
                    act.wait_ge(ps_ready["L"], count(use))
                    act.activation(graph[:, i, b, 0:(i + 1) * P], slot(use)[:, 0:(i + 1) * P], ACT.Copy,
                                   scale=rule[:, 4, i % 2, b:b + 1], saturate=False).then_inc(ps_free["L"], 1)
                elif kind == "M":
                    act.wait_ge(ps_ready["M"], count(("M", i, b)))
                    act.activation(graph[:, 0:i + 1, b, i * P:(i + 1) * P],
                                   slot(("M", i, b))[:, 0:(i + 1) * P].rearrange("p (j c) -> p j c", j=i + 1),
                                   ACT.Sign, saturate=False).then_inc(ps_free["M"], 1)
                elif kind == "H":
                    act.wait_ge(ln_var, b + 1)
                    act.activation(ln_std[:, 1, :], ln_std[:, 0, :], ACT.Sqrt).then_inc(ln_root, 1)
                    act.wait_ge(ps_ready["H"], b + 1)
                    act.activation(rT[:, b, :], slot(("H", 0, b)), ACT.Relu).then_inc(ps_free["H"], 1)

            def top(l, b):
                act.wait_ge(prod_free, (l * NB + b + 1) * 4)
                act.activation(parts[:, b % 2, :, 0:D], zo[:, b % 2, :, 0:D], ACT.Copy).then_inc(top_ready, 1)

            def lengths(l, b):
                n = l * NB + b
                for t in range(NT):
                    if t % 2 == 0:
                        act.wait_ge(sage_ready, n * NT + t + 2)
                    act.activation(squares[:, t * D:(t + 1) * D], sage[:, b % 2, t, :], ACT.Square,
                                   accum_out=norms[:, 0, t:t + 1]).then_inc(squared, 1)
                act.wait_ge(squared, (n + 1) * NT)
                act.activation(norms[:, 1, :], norms[:, 0, :], ACT.Sqrt).then_inc(root_ready, 1)

            def turn_out(l, b):
                n = l * NB + b
                act.wait_ge(turn_ready, n + 1)
                act.activation(rT[:, b, :], turn_ps, ACT.Relu, accum_out=moments[:, 0, b:b + 1]
                               ).then_inc(moments_ready, 1)
                act.wait_ge(moments_ready, 2 * n + 1)
                act.activation(squares, rT[:, b, :], ACT.Square, accum_out=moments[:, 1, b:b + 1]
                               ).then_inc(moments_ready, 1)
                act.wait_ge(moments_ready, 2 * n + 2)

            act.wait_ge(pool_step, 10 + 1 + NT + 1)
            with act.Fori(0, LAYERS) as l:
                top(l, 0)
                top(l, 1)
                for b in range(NB):
                    lengths(l, b)
                    if b + 2 < NB:
                        top(l, b + 2)
                    if b:
                        turn_out(l, b - 1)
                turn_out(l, NB - 1)
                act.wait_ge(bn_var, l + 1)
                act.activation(bn[:, 7:8], bn[:, 6:7], ACT.Sqrt).then_inc(bn_root, 1)
            for b in range(NB):
                act.wait_ge(last_step, b + 1)
                for t in range(NT):
                    act.activation(ysum[:, b, t, :], ysum[:, b, t, :], ACT.Copy,
                                   scale=columns[:, b * NT + t:b * NT + t + 1]).then_inc(scaled, 1)

        @block.tensor
        def _(pe):
            def mm(out_, lhsT, rhs, start, stop):
                return pe.matmul(out_, lhsT, rhs, start=start, stop=stop)

            pe.wait_ge(consts_made, 7)
            pe.wait_ge(rows_ready, 1)
            pe.wait_ge(params_in, 16 * 2 * LAYERS)
            nv = NB * NT + 2 * LAYERS
            mm(spare[:, 0:nv], vectors[:, :], eye32[0:nv, 0:nv], True, True).then_inc(columns_ps, 1)

            def ready_slot(use):
                old = BEFORE[use]
                if old:
                    pe.wait_ge(ps_free[old[0]], count(old))

            def original(i, j, b):
                return diag_low[:, i % 2, b, :] if i == j else graph[:, j, b, i * P:(i + 1) * P]

            def prefix(ps, tiles, width):
                for first, (at, tile) in enumerate(tiles):
                    for lo, hi in pieces(at, width):
                        last = mm(ps[:, lo:hi], tile, stair[:, lo - at:hi - at], first == 0,
                                  at + P >= min(width, (lo // BANK + 1) * BANK))
                return last

            def minus(ps, marks, width):
                for row in marks:
                    for lo, hi in pieces(0, width):
                        last = mm(ps[:, lo:hi], neg_eye[:, :], row[:, lo:hi], False, row is marks[-1])
                return last

            def upper_ranks(i, b):
                use = ("C", i, b)
                ready_slot(use)
                pe.wait_ge(triangles_ready, 2 * (i + 1))
                prefix(slot(use), [((j - i) * P, original(i, j, b)) for j in range(i, NT)],
                       N - i * P).then_inc(ps_ready["C"], 1)

            def block_counts(i):
                pe.wait_ge(triangles_ready, 2 * (i + 1))
                if i:
                    pe.wait_ge(final_step, i * CODES)
                mm(removed, eye[:, :], zeros[:, :], True, False)
                for b in range(NB):
                    if i:
                        pe.wait_ge(ps_free["P"], (i - 1) * NB + b + 1)
                    col = counts[:, NB + b:NB + b + 1]
                    for j in range(i):
                        mm(col, graph[:, j, b, i * P:(i + 1) * P], ones[:, :], False, False)
                    mm(col, diag_up[:, i % 2, b, :], ones[:, :], False, False)
                    col = counts[:, 2 * NB + b:2 * NB + b + 1]
                    for j in range(i, NT):
                        last = mm(col, original(i, j, b), ones[:, :], False, j == NT - 1 and b == NB - 1)
                last.then_inc(removed_ready, 1)

            def count_removed(i, done, at):
                pe.wait_ge(done, at)
                for b in range(NB):
                    mm(removed[:, b:b + 1], diag_up[:, i % 2, b, :], small[:, b:b + 1], b == 0, False)
                for b in range(NB):
                    mm(removed[:, b:b + 1], last_edge[:, :, b], even[:, b:b + 1], False, False)
                for b in range(NB):
                    last = mm(removed[:, b:b + 1], hit[:, :, b], ones[:, :], False, b == NB - 1)
                return last

            def count_changes(i):
                g = sweep_number(i, SWEEPS[i])
                pe.wait_ge(sweep_step, STEPS * g + HIT)
                if i:
                    pe.wait_ge(flag_ready, i)
                pe.matmul(spare[0:1, 0:NB], ones[:, :], changed[:, :], start=True, stop=True).then_inc(flag_ps, 1)

            def test(i):
                pe.wait_ge(flag_ready, i + 1)
                more = pe.value_load(flag[0:1, 0:1], min_val=0, max_val=P)
                with pe.If(more > 0):
                    with pe.Fori(0, P) as k:
                        count_removed(i, more_step[i], (k + 1) * STEPS).then_inc(more_removed[i], 1)

            def rows_after(i, b):
                use = ("P", i, b)
                ready_slot(use)
                ps, width = slot(use), N - i * P
                for j in range(i, NT):
                    at = (j - i) * P
                    mm(ps[:, at:at + P], original(i, j, b), eye[:, :], at % BANK == 0, False)
                pe.wait_ge(hits_up, 2 * (i * NB + b + 1))
                minus(ps, hits("U", b), width).then_inc(ps_ready["P"], 1)

            def lower_ranks(i, b):
                use = ("V", i, b)
                ready_slot(use)
                pe.wait_ge(ps_free["P"], i * NB + b + 1)
                prefix(slot(use), [(j * P, graph[:, j, b, i * P:(i + 1) * P]) for j in range(i + 1)],
                       (i + 1) * P).then_inc(ps_ready["V"], 1)

            def kept(i, b):
                use = ("L", i, b)
                ready_slot(use)
                ps, width = slot(use), (i + 1) * P
                for j in range(i + 1):
                    mm(ps[:, j * P:(j + 1) * P], graph[:, j, b, i * P:(i + 1) * P], eye[:, :],
                       j * P % BANK == 0, False)
                pe.wait_ge(hits_low, i * NB + b + 1)
                minus(ps, hits("L", b), width).then_inc(ps_ready["L"], 1)

            def mirror(i, b):
                use = ("M", i, b)
                ready_slot(use)
                pe.wait_ge(ps_free["L"], i * NB + b + 1)
                ps = slot(use)
                for j in range(i + 1):
                    mm(ps[:, j * P:(j + 1) * P], graph[:, i, b, j * P:(j + 1) * P], eye[:, :],
                       j * P % BANK == 0, j < i and (j + 1) * P % BANK == 0)
                mm(ps[:, i * P:(i + 1) * P], eye[:, :], graph[:, i, b, i * P:(i + 1) * P], False, True
                   ).then_inc(ps_ready["M"], 1)

            for kind, i, b in TASKS:
                if kind == "C":
                    upper_ranks(i, b)
                elif kind == "S":
                    block_counts(i)
                elif kind == "W":
                    g = sweep_number(i, b)
                    count_removed(i, sweep_step, STEPS * (g + 1)).then_inc(removed_ready, 1)
                elif kind == "F":
                    count_changes(i)
                elif kind == "T":
                    test(i)
                elif kind == "P":
                    rows_after(i, b)
                elif kind == "V":
                    lower_ranks(i, b)
                elif kind == "L":
                    kept(i, b)
                elif kind == "M":
                    mirror(i, b)
                elif kind == "H":
                    use = ("H", 0, b)
                    ready_slot(use)
                    pe.wait_ge(ln_done, (b + 1) * NT)
                    for t in range(NT):
                        last = pe.transpose(slot(use)[:, t * P:(t + 1) * P], rT[:, b, t * P:(t + 1) * P],
                                            eye32[:, :])
                    last.then_inc(ps_ready["H"], 1)

            for l in range(LAYERS):
                pe.wait_ge(reach_made, 3 * (l + 1))
                if l:
                    pe.wait_ge(reach_step, 6 + 5 * l)
                mm(spare[:, D:2 * D], reach_wide[:, :], wabs[:, :], True, True).then_inc(reach_ps, 1)

            for k in "CPVLMH":
                pe.wait_ge(ps_free[k], NB if k == "H" else NT * NB)

            def products(l, b, first):
                for t in range(NT):
                    n = (l * NB + b) * 4 + t // 2
                    k = (t // 2) % 2
                    if t % 2 == 0 and (b or t >= 4):
                        if b >= 4 and t < 4 and not first:
                            pe.wait_ge(y_added, ((l - 1) * NB + b - 4) * 2 + k + 1)
                        else:
                            pe.wait_ge(prod_free, n - 1)
                    last = mm(prod_ps[k][:, (t % 2) * 2 * D:(t % 2 + 1) * 2 * D],
                              rT[:, b, t * P:(t + 1) * P], wscaled[:, 0:2 * D], True, True)
                    if t % 2:
                        last.then_inc(prod_ready, 1)

            def aggregate(l, b):
                pe.wait_ge(low_ready, l * NB + b + 1)
                for k in range(4):
                    n = (l * NB + b) * 4 + k
                    if b or k >= 2:
                        pe.wait_ge(sage_ready, 2 * (n - 1))
                    mm(agg_ps[:, k % 2, 0, 0:1], eye[:, :], ones[:, :], True, True)
                    for h in range(2):
                        t = 2 * k + h
                        for j in range(NT):
                            last = mm(agg_ps[:, k % 2, h, 0:WZ], graph[:, j, b, t * P:(t + 1) * P],
                                      parts[:, b % 2, j, 0:WZ], j == 0, j == NT - 1)
                    last.then_inc(agg_ready, 1)

            def turn(l, b):
                n = l * NB + b
                pe.wait_ge(unit_ready, n + 1)
                if b:
                    pe.wait_ge(moments_ready, 2 * n)
                for t in range(NT):
                    last = pe.transpose(turn_ps[:, t * P:(t + 1) * P], sage[:, b % 2, t, :], eye32[:, :])
                last.then_inc(turn_ready, 1)

            def head_rows(l, b, after_products):
                for h in range(2):
                    if after_products:
                        pe.wait_ge(prod_free, ((l + 1) * NB + b + 3) * 4 + 3 + h)
                    elif b:
                        pe.wait_ge(y_added, (l * NB + b - 1) * 2 + h + 1)
                    for t in range(4):
                        last = mm(prod_ps[h][:, t * D:(t + 1) * D],
                                  rT[:, b, (4 * h + t) * P:(4 * h + t + 1) * P],
                                  wscaled[:, 2 * D:3 * D], True, True)
                    last.then_inc(y_ps, 1)

            def layer(l, first):
                pe.wait_ge(wide_ready, 2 * (l + 1))
                width = 2 * D if first else 3 * D
                mm(prod_ps[0][:, 0:width], shift_wide[:, :], wcur[:, 0:width], True, True
                   ).then_inc(rowconst_ps, 1)
                if not first:
                    pe.wait_ge(head_step, 2 * l)
                pe.wait_ge(prep_step, 2 + 4 * (l + 1))
                products(l, 0, first)
                products(l, 1, first)
                for b in range(NB):
                    aggregate(l, b)
                    if b + 2 < NB:
                        products(l, b + 2, first)
                    if b:
                        if not first:
                            head_rows(l - 1, b - 1, b + 2 < NB)
                        turn(l, b - 1)
                if not first:
                    head_rows(l - 1, NB - 1, False)
                turn(l, NB - 1)

            layer(0, True)
            with pe.Fori(1, LAYERS) as l:
                layer(l, False)
            l = LAYERS - 1
            pe.wait_ge(wide_ready, 2 * (LAYERS + 1))
            mm(prod_ps[0][:, 2 * D:3 * D], shift_wide[:, :], wcur[:, 2 * D:3 * D], True, True
               ).then_inc(rowconst_ps, 1)
            pe.wait_ge(head_step, 2 * LAYERS)
            for b in range(NB):
                head_rows(l, b, False)


_OUT = (NB, N, D)


def kernel(**inputs):
    import numpy as np
    import concourse.bacc as bacc
    from concourse.bass_utils import run_bass_kernel_spmd as run

    nc = bacc.Bacc("TRN2", target_bir_lowering=False, num_devices=1)
    arrays, aps = {}, {}
    for name, value in inputs.items():
        a = np.ascontiguousarray(value)
        arrays[f"in_{name}"] = a
        aps[name] = nc.dram_tensor(f"in_{name}", a.shape, mybir.dt.from_np(a.dtype), kind="ExternalInput").ap()
    result = nc.dram_tensor("result", _OUT, F32, kind="ExternalOutput").ap()

    def each(stem):
        return [aps[f"L0_gnn_{stem}{l}"] for l in (1, 2, 3)]

    build(nc, aps["x"], aps["adj"], aps["nodemask"], each("Wr"), each("Wx"), each("b"), each("g"),
          each("be"), aps["L0_gnn_Wl"], aps["L0_gnn_bl"], result)
    return run(nc, [arrays], core_ids=[0]).results[0]["result"]
```

```python
from contextlib import ExitStack

import concourse.bass as bass
from concourse import mybir

F32, BF16, F16 = mybir.dt.float32, mybir.dt.bfloat16, mybir.dt.float16
F8, I32 = mybir.dt.float8e4, mybir.dt.int32
ALU, ACT, AX = mybir.AluOpType, mybir.ActivationFunctionType, mybir.AxisListType

P = 128
NB, N, D = 8, 1024, 128
NT = N // P
LAYERS = 3
BANK = 512

EDGE = 2048.0
SHIFT = 1024.0
NEVER = 4096.0
FAR = 9000.0
ALL = 1000.0
ROUND = 1.5 * 2.0 ** 23
SWEEPS = [3, 6, 6, 5, 4, 4, 5, 6]
STEPS = 9
SETUP = 8
CODES = 11
GAP, FEW, HALF, SOME, CODE, PARITY, SMALL, HIT, EVEN = range(1, STEPS + 1)

AHEAD = 3
BESIDE_SWEEP, BESIDE_TEST, BESIDE_SETUP = 1.9, 2.5, 1.5
FIRST_LOWER = 14
ACT_TILES = 4
EARLY = 4
TURN_BLOCKS = 3
RING = 6
WZ = 2 * P + 1
TOP = 2.0 ** 14
ZROW = WZ + 1
BN_EPS, LN_EPS, NORM_EPS = 1e-5, 1e-5, 1e-12


def pieces(lo, hi):
    cuts = [lo] + [c for c in range(BANK, N, BANK) if lo < c < hi] + [hi]
    return list(zip(cuts[:-1], cuts[1:]))


def lower_tasks(i):
    return [task for b in range(NB + 3)
            for task in (("V", i, b), ("K", i, b - 1), ("L", i, b - 2), ("M", i, b - 3)) if 0 <= task[2] < NB]


def order():
    tasks = [("N", 0, b) for b in range(EARLY)]
    for b in range(NB):
        tasks += [("C", 0, b)] + ([("N", 0, EARLY + b // 2)] if b % 2 == 0 and EARLY + b // 2 < NB else [])
    tasks += [("U", 0, 0), ("Z", 0, 0)]
    turns = [("H", 0, b) for b in range(NB)]
    for i in range(NT):
        lower = lower_tasks(i - 1) if i else []
        upper = [("C", i + 1, b) for b in range(NB)] if i + 1 < NT else []
        jobs = lower[:FIRST_LOWER] + upper + lower[FIRST_LOWER:]
        if i < TURN_BLOCKS:
            jobs += turns[i * NB // TURN_BLOCKS:(i + 1) * NB // TURN_BLOCKS]
        tasks.append(("S", i, 0))
        tasks += take(jobs, BESIDE_SETUP)
        for k in range(SWEEPS[i]):
            tasks.append(("W", i, k))
            tasks += take(jobs, BESIDE_SWEEP)
        tasks.append(("F", i, 0))
        tasks += take(jobs, BESIDE_TEST)
        tasks.append(("T", i, 0))
        for b in range(NB):
            tasks.append(("P", i, b))
            if b == 1 and i + 1 < NT:
                tasks.append(("U", i + 1, 0))
            tasks += take(jobs, work(jobs) / (NB - b))
        if i + 1 < NT:
            tasks.append(("Z", i + 1, 0))
    rest = lower_tasks(NT - 1)
    for l in range(LAYERS):
        for at, kind in ((3, "Q"), (6, "R"), (9, "B")):
            rest.insert(10 * l + at, (kind, l, 0))
    return tasks + rest


def cost(task):
    kind, i, b = task
    tiles = NT - i if kind == "C" else i + 1
    return {"C": 0.053 * tiles * (tiles + 1) / 2, "V": 0.053 * tiles * (tiles + 1) / 2,
            "K": 0.0, "L": 0.053 * 2 * tiles, "M": 0.053 * (tiles + 1), "H": 1.7}[kind]


def work(jobs):
    return sum(map(cost, jobs))


def take(jobs, most):
    out, total = [], 0.0
    while jobs and total + cost(jobs[0]) / 2 < most:
        total += cost(jobs[0])
        out.append(jobs.pop(0))
    return out


TASKS = order()
USES = [task for task in TASKS if task[0] in "CPVLMH"]
SLOT, BEFORE = {}, {}


def banks(use):
    kind, i, b = use
    tiles = NT if kind == "H" else NT - i if kind in "CP" else i + 1
    return -(-tiles * P // BANK)


def place():
    at, holder = 0, [None] * RING
    for use in USES:
        if at + banks(use) > RING:
            at = 0
        SLOT[use] = at
        BEFORE[use] = [old for old in dict.fromkeys(holder[at:at + banks(use)]) if old]
        holder[at:at + banks(use)] = [use] * banks(use)
        at = (at + banks(use)) % RING


place()


def count(use):
    kind, i, b = use
    return i * NB + b + 1


def sweep_number(i, k):
    return sum(SWEEPS[:i]) + i + k


def build(nc, x, adj, nodemask, wr, wx, bias, gain, shift, wl, bl, out):
    with ExitStack() as ctx:
        def sb(name, shape, dt):
            return ctx.enter_context(nc.sbuf_tensor(name, shape, dt))

        def pb(name, shape, dt=F32):
            return ctx.enter_context(nc.psum_tensor(name, shape, dt))

        def sem(name):
            return ctx.enter_context(nc.semaphore(name))

        graph = sb("graph", [P, NT, NB, N], F8)
        codes = sb("codes", [P, 2 * NB * N], F16)
        ranks = codes[:, :].rearrange("p (q b m) -> p q b m", q=2, b=NB)
        ysum = codes[:, :].bitcast(F32).rearrange("p (b t d) -> p b t d", b=NB, t=NT)
        rT = sb("rT", [P, NB, N], F32)
        arena = sb("arena", [P, 13 * N], F32)
        taken = [0]

        def cut(words, dt=F32):
            taken[0] += words
            piece = arena[:, taken[0] - words:taken[0]]
            return piece if dt == F32 else piece.bitcast(dt)

        hit_rows = cut(4 * N, BF16).rearrange("p (k q m) -> p k q m", k=4, q=2)
        low_codes = cut(N, F16).rearrange("p (q m) -> p q m", q=2)
        diag_codes = cut(N, F16).rearrange("p (q m b) -> p q m b", q=2, b=NB)
        hit = cut(N // 2, BF16).rearrange("p (m b) -> p m b", b=NB)
        last_edge = cut(N // 2, BF16).rearrange("p (m b) -> p m b", b=NB)
        diag_low = cut(N, BF16).rearrange("p (q b c) -> p q b c", q=2, b=NB)
        diag_up = cut(N, BF16).rearrange("p (q b c) -> p q b c", q=2, b=NB)
        taken[0] = 0
        zo = cut(4 * N).rearrange("p (q t c) -> p q t c", q=2, t=NT)
        parts = cut(NT * ZROW, F16).rearrange("p (q t c) -> p q t c", q=2, t=NT)
        sage = cut(2 * N).rearrange("p (q t d) -> p q t d", q=2, t=NT)
        squares = cut(N // 2, BF16)
        part_sum = cut(4 * D).rearrange("p (q t d) -> p q t d", q=2, t=2)
        shift_wide = cut(P)
        rowconst = cut(2 * D)
        wcur = cut(3 * D)
        wscaled = cut(3 * D)
        xin = sb("xin", [P, 2, NT, D], F32)
        x_again = ([xin[:, b, :, :] for b in range(2)]
                   + [arena[:, b * N:(b + 1) * N].rearrange("p (t d) -> p t d", t=NT) for b in range(4)]
                   + [sage[:, b, :, :] for b in range(2)])
        stair = sb("stair", [P, N], BF16)
        eye = sb("eye", [P, P], BF16)
        neg_eye = sb("neg_eye", [P, P], BF16)
        off_eye = sb("off_eye", [P, P], F16)
        low_mask = sb("low_mask", [P, P], F32)
        up_mask = sb("up_mask", [P, P], F32)
        eye32 = sb("eye32", [P, P], F32)
        ones = sb("ones", [P, 1], BF16)
        zeros = sb("zeros", [P, NB], BF16)
        mask_rows = sb("mask_rows", [NB * NT, P], I32)
        vectors = sb("vectors", [NB * NT + 2 * LAYERS, P], F32)
        columns = sb("columns", [P, NB * NT + 2 * LAYERS], F32)
        mask = columns[:, 0:NB * NT].rearrange("p (b t) -> p b t", b=NB)
        live = sb("live", [P, NB, NT], F32)
        half_right = sb("half_right", [P, NB], F32)
        gap0, few_at, some_at, last_at = (sb(n, [P, NB], F32) for n in
                                          ("gap0", "few_at", "some_at", "last_at"))
        last_code = sb("last_code", [P, NB], F16)
        gap = sb("gap", [P, 2, NB], F32)
        few, half, some, parity = (sb(n, [P, NB], F32) for n in ("few", "half", "some", "parity"))
        code = sb("code", [P, NB], F16)
        small, even, changed = (sb(n, [P, NB], BF16) for n in ("small", "even", "changed"))
        flag = sb("flag", [1, 1], I32)
        edge_a, edge_b, left = (sb(n, [P, NB], F32) for n in ("edge_a", "edge_b", "left"))
        left_low = sb("left_low", [P, NB], F32)
        rule = sb("rule", [P, 5, 2, NB], F32)
        mid_a, mid_b, mid_c = (sb(n, [P, NB], F32) for n in ("mid_a", "mid_b", "mid_c"))
        ln_stats, ln_mv = sb("ln_stats", [P, NT, 6], F32), sb("ln_mv", [P, 2, NT, 2], F32)
        ln_std, ln_inv = sb("ln_std", [P, 2, NT], F32), sb("ln_inv", [P, 2, 2, NT], F32)
        zback = sb("zback", [P, 1], F32)
        wabs = sb("wabs", [P, D], F32)
        reach = sb("reach", [P, 3, LAYERS], F32)
        reach_wide = sb("reach_wide", [P, P], F32)
        zscale = sb("zscale", [P, 2, LAYERS], F32)
        wraw = sb("wraw", [P, LAYERS, 3 * D], F32)
        bias_wide = sb("bias_wide", [P, LAYERS, 2 * D], F32)
        head_const = sb("head_const", [P, D], F32)
        degree = sb("degree", [P, 2, 2], F32)
        norms = sb("norms", [P, 4, NT], F32)
        moments = sb("moments", [P, 2, NB], F32)
        bn = sb("bn", [P, 10], F32)
        affine = sb("affine", [P, 2], F32)

        ring = pb("ring", [P, RING * BANK])
        counts = pb("counts", [P, BANK])
        spare = pb("spare", [P, BANK])
        removed, left_ps, right_ps = counts[:, 0:NB], counts[:, NB:2 * NB], spare[:, NB:2 * NB]
        agg_ps = ring[:, 0:4 * BANK].rearrange("p (s k c) -> p s k c", s=2, k=2)
        turn_ps = ring[:, 4 * BANK:6 * BANK]
        prod_ps = [counts, spare]

        adj_in = [sem(f"adj_in{i}") for i in range(NT)]
        x_in = [sem(f"x_in{b}") for b in range(NB)]
        params_in, mask_in, weights_in = sem("params_in"), sem("mask_in"), sem("weights_in")
        consts_made, rows_ready = sem("consts_made"), sem("rows_ready")
        cut_step = sem("cut_step")
        pool_step, triangles_ready, diag_codes_ready = sem("pool_step"), sem("triangles_ready"), sem("diag_codes_ready")
        columns_ps, columns_ready = sem("columns_ps"), sem("columns_ready")
        ps_ready = {k: sem(f"ps_ready_{k}") for k in "CPVLMH"}
        ps_free = {k: sem(f"ps_free_{k}") for k in "CPVLMH"}
        removed_ready = sem("removed_ready")
        right_ready, setup_step, level_step, sweep_step = (
            sem(n) for n in ("right_ready", "setup_step", "level_step", "sweep_step"))
        final_step, changed_ready, flag_ps, flag_ready = (
            sem(n) for n in ("final_step", "changed_ready", "flag_ps", "flag_ready"))
        more_step = [sem(f"more_step{i}") for i in range(NT)]
        more_removed = [sem(f"more_removed{i}") for i in range(NT)]
        hits_up, hits_low = sem("hits_up"), sem("hits_low")
        ln_stat, ln_var, ln_root, ln_scale, ln_done = (
            sem(n) for n in ("ln_stat", "ln_var", "ln_root", "ln_scale", "ln_done"))
        ln_done_dve = sem("ln_done_dve")
        reach_step, reach_made, reach_ps = sem("reach_step"), sem("reach_made"), sem("reach_ps")
        prep_step, wide_ready, rowconst_ps = sem("prep_step"), sem("wide_ready"), sem("rowconst_ps")
        prod_ready, prod_free = sem("prod_ready"), sem("prod_free")
        top_ready, low_ready = sem("top_ready"), sem("low_ready")
        agg_ready, sage_step, sage_ready = sem("agg_ready"), sem("sage_step"), sem("sage_ready")
        squared, root_ready, norm_step, unit_ready = (
            sem(n) for n in ("squared", "root_ready", "norm_step", "unit_ready"))
        turn_ready, turned, moments_ready = sem("turn_ready"), sem("turned"), sem("moments_ready")
        bn_step, bn_var, bn_root, head_step = (sem(n) for n in ("bn_step", "bn_var", "bn_root", "head_step"))
        y_ps, y_added = sem("y_ps"), sem("y_added")
        last_step, again_in, stored = (
            sem("last_step"), [sem(f"again_in{b}") for b in range(NB)], sem("stored"))
        ysum_cleared, scaled = sem("ysum_cleared"), sem("scaled")
        out_ready = sem("out_ready")

        def slot(use):
            return ring[:, SLOT[use] * BANK:(SLOT[use] + banks(use)) * BANK]

        def hits(kind, b):
            return [hit_rows[:, k, b % 2, :] for k in ((0, 1) if kind == "U" else (2,))]

        def product_bank(k, beside_head):
            return prod_ps[k // 3 if beside_head else k % 2]

        def head_bank(h, beside_products):
            return prod_ps[1 if beside_products else 1 - h]

        block = ctx.enter_context(nc.Block())

        @block.sync
        def _(sp):
            sp.dma_start(mask_rows[:, :], nodemask.rearrange("b (t p) -> (b t) p", p=P)).then_inc(mask_in, 16)
            for l in range(LAYERS):
                r = NB * NT + l
                sp.dma_start(vectors[r:r + 1, :], gain[l].unsqueeze(0)).then_inc(params_in, 16)
                sp.dma_start(vectors[r + LAYERS:r + LAYERS + 1, :], shift[l].unsqueeze(0)).then_inc(params_in, 16)
            for b in range(NB):
                if b == EARLY:
                    sp.wait_ge(adj_in[0], 16 * NB)
                sp.dma_start(rT[:, b, :].rearrange("p (t d) -> p t d", t=NT),
                             x[b].rearrange("(t p) d -> p t d", p=P)).then_inc(x_in[b], 16)
            for l in range(LAYERS):
                for k, w in enumerate((wr, wx, wl)):
                    src = w[l] if k < 2 else wl[l * D:(l + 1) * D, :]
                    sp.dma_start(wraw[:, l, k * D:(k + 1) * D], src).then_inc(weights_in, 16)
                sp.dma_start(bias_wide[:, l, D:2 * D], bias[l].unsqueeze(0).broadcast_to([P, D])
                             ).then_inc(weights_in, 16)
            sp.dma_start(head_const[:, :], bl.unsqueeze(0).broadcast_to([P, D])).then_inc(weights_in, 16)
            for b in range(NB):
                if b == 2:
                    sp.wait_ge(sage_ready, LAYERS * NB * NT)
                    sp.wait_ge(low_ready, LAYERS * NB)
                elif b == 6:
                    sp.wait_ge(turn_ready, LAYERS * NB)
                sp.dma_start(x_again[b], x[b].rearrange("(t p) d -> p t d", p=P)).then_inc(again_in[b], 16)
            for b in range(NB):
                sp.wait_ge(out_ready, b + 1)
                sp.dma_start(out[b].rearrange("(t p) d -> p t d", p=P), x_again[b]).then_inc(stored, 16)
            sp.wait_ge(stored, 16 * NB)

        @block.gpsimd
        def _(pool):
            def load(i, b):
                tiles = adj[b, i * P:N, i * P:(i + 1) * P].rearrange("(j p) c -> p j c", p=P)
                pool.dma_start(graph[:, i:NT, b, i * P:(i + 1) * P], tiles).then_inc(adj_in[i], 16)

            def load_strip(i):
                for b in range(NB):
                    load(i, b)

            load_strip(0)
            made = 0
            for tile, value in ((eye[:, :], 0.0), (neg_eye[:, :], 0.0), (eye32[:, :], 0.0),
                                (off_eye[:, :], 1.0), (stair[:, :], 1.0), (low_mask[:, :], 1.0),
                                (up_mask[:, :], 1.0), (ones[:, :], 1.0), (zeros[:, :], 0.0),
                                (bias_wide[:, :, 0:D], 0.0)):
                made += 1
                pool.memset(tile, value).then_inc(pool_step, 1)
            pool.wait_ge(pool_step, made)

            def select(tile, op, fill, sign):
                return pool.affine_select(out=tile, in_=tile, compare_op=op, fill=fill, base=0,
                                          pattern=[[sign, P]], channel_multiplier=-sign)

            select(eye[:, :], ALU.not_equal, 1.0, 1).then_inc(consts_made, 1)
            select(neg_eye[:, :], ALU.not_equal, -1.0, 1).then_inc(consts_made, 1)
            select(eye32[:, :], ALU.not_equal, 1.0, 1).then_inc(consts_made, 1)
            select(off_eye[:, :], ALU.not_equal, 0.0, 1).then_inc(consts_made, 1)
            select(low_mask[:, :], ALU.is_ge, 0.0, -1).then_inc(consts_made, 1)
            select(up_mask[:, :], ALU.is_gt, 0.0, 1).then_inc(consts_made, 1)
            select(stair[:, 0:P], ALU.is_ge, 0.0, 1).then_inc(pool_step, 1)
            pool.wait_ge(pool_step, made + 1)
            select(stair[:, 0:P], ALU.not_equal, EDGE, 1).then_inc(consts_made, 1)
            pool.wait_ge(consts_made, 7)
            def triangles(i):
                pool.wait_ge(adj_in[i], 16 * NB)
                if i >= 2:
                    pool.wait_ge(ps_ready["P"], (i - 1) * NB)
                diag = graph[:, i, :, i * P:(i + 1) * P]
                for tile, mask_ in ((diag_low, low_mask), (diag_up, up_mask)):
                    pool.tensor_tensor(tile[:, i % 2, :, :], diag,
                                       mask_[:, :].unsqueeze(1).broadcast_to([P, NB, P]),
                                       ALU.mult).then_inc(triangles_ready, 1)

            def diagonal_codes(i, b):
                pool.wait_ge(ps_free["C"], i * NB + b + 1)
                d = ranks[:, i % 2, b, 0:P]
                pool.tensor_tensor(d, d, off_eye[:, :], ALU.mult).then_inc(cut_step, 1)
                pool.wait_ge(cut_step, i * NB + b + 1)
                if i >= 2 and b == 0:
                    pool.wait_ge(final_step, (i - 1) * CODES)
                pool.tensor_copy(diag_codes[:, i % 2, :, b], d).then_inc(diag_codes_ready, 1)

            triangles(0)
            load_strip(1)
            for kind, i, b in TASKS:
                if kind == "C":
                    diagonal_codes(i, b)
                elif kind == "U" and i == 0:
                    triangles(1)
                    load_strip(2)
                elif kind == "P":
                    if i + AHEAD < NT:
                        load(i + AHEAD, b)
                    if b == NB - 1 and i + 2 < NT:
                        triangles(i + 2)
            for k in "CPVLMH":
                pool.wait_ge(ps_free[k], NB if k == "H" else NT * NB)
            pool.memset(parts[:, :, :, 2 * D:WZ], 1.0).then_inc(pool_step, 1)
            pool.wait_ge(pool_step, made + 2)

            def low(l, b):
                pool.wait_ge(top_ready, l * NB + b + 1)
                pool.tensor_tensor(parts[:, b % 2, :, D:2 * D], zo[:, b % 2, :, 0:D],
                                   parts[:, b % 2, :, 0:D], ALU.subtract).then_inc(low_ready, 1)

            for b in range(NB):
                low(0, b)
                if b == 1:
                    pool.wait_ge(hits_up, 2 * NT * NB)
                    pool.memset(ysum[:, :, :, :].rearrange("p b t d -> p (b t d)"), 0.0).then_inc(ysum_cleared, 1)
            with pool.Fori(1, LAYERS) as l:
                for b in range(NB):
                    low(l, b)
            for b in range(NB):
                pool.wait_ge(again_in[b], 16)
                pool.wait_ge(scaled, (b + 1) * NT)
                pool.tensor_tensor(x_again[b], x_again[b], ysum[:, b, :, :], ALU.add).then_inc(out_ready, 1)

        @block.vector
        def _(dve):
            dve.wait_ge(mask_in, 16)
            dve.tensor_copy(vectors[0:NB * NT, :], mask_rows[:, :]).then_inc(rows_ready, 1)

            def mask_columns():
                dve.wait_ge(columns_ps, 1)
                dve.tensor_copy(columns[:, :], spare[:, 0:NB * NT + 2 * LAYERS]).then_inc(columns_ready, 1)
                dve.wait_ge(columns_ready, 1)
                dve.tensor_scalar(live[:, :, :], mask, 0.0, None, ALU.not_equal).then_inc(columns_ready, 1)
                dve.wait_ge(columns_ready, 2)

            def setup(i):
                n = i * SETUP
                alive = live[:, :, i]
                dve.wait_ge(right_ready, i + 1)
                dve.tensor_scalar(half_right[:, :], right_ps, 0.5, 0.25, ALU.mult, ALU.add).then_inc(setup_step, 1)
                dve.scalar_tensor_tensor(few_at[:, :], right_ps, FAR - 5.0, alive, ALU.add, ALU.mult
                                         ).then_inc(setup_step, 1)
                dve.scalar_tensor_tensor(some_at[:, :], right_ps, FAR - 0.5, alive, ALU.add, ALU.mult
                                         ).then_inc(setup_step, 1)
                dve.tensor_scalar(last_at[:, :], right_ps, -1.0, FAR - SHIFT + 1.0, ALU.mult, ALU.add
                                  ).then_inc(setup_step, 1)
                dve.tensor_scalar(last_code[:, :], right_ps, SHIFT - 1.0, None, ALU.add).then_inc(setup_step, 1)
                dve.wait_ge(setup_step, n + 5)
                dve.tensor_scalar(few_at[:, :], few_at[:, :], -FAR, None, ALU.add).then_inc(setup_step, 1)
                dve.tensor_scalar(some_at[:, :], some_at[:, :], -FAR, None, ALU.add).then_inc(setup_step, 1)
                dve.wait_ge(diag_codes_ready, (i + 1) * NB)
                dve.tensor_tensor(last_edge[:, :, :], diag_codes[:, i % 2, :, :],
                                  last_code[:, :].unsqueeze(1).broadcast_to([P, P, NB]),
                                  ALU.is_equal).then_inc(setup_step, 1)

            def level(i):
                dve.wait_ge(removed_ready, sweep_number(i, 0) + 1)
                dve.wait_ge(setup_step, (i + 1) * SETUP)
                dve.scalar_tensor_tensor(gap0[:, :], left_ps, -0.5, half_right[:, :], ALU.mult, ALU.add
                                         ).then_inc(level_step, 1)
                dve.tensor_scalar(left_low[:, :], left_ps, EDGE - SHIFT, None, ALU.add).then_inc(level_step, 1)
                dve.wait_ge(level_step, 2 * (i + 1))

            def sweep(i, gap_now, done, at, with_hits):
                dve.scalar_tensor_tensor(gap_now, removed, 0.5, gap0[:, :], ALU.mult, ALU.add).then_inc(done, 1)
                dve.wait_ge(done, at + GAP)
                dve.tensor_tensor(few[:, :], gap_now, few_at[:, :], ALU.is_ge).then_inc(done, 1)
                dve.tensor_scalar(half[:, :], gap_now, ROUND, ROUND - SHIFT + 1.0, ALU.add,
                                  ALU.subtract).then_inc(done, 1)
                dve.tensor_tensor(some[:, :], gap_now, some_at[:, :], ALU.is_lt).then_inc(done, 1)
                dve.wait_ge(done, at + HALF)
                dve.scalar_tensor_tensor(code[:, :], few[:, :], NEVER, half[:, :], ALU.mult,
                                         ALU.max).then_inc(done, 1)
                dve.tensor_tensor(parity[:, :], gap_now, half[:, :], ALU.subtract).then_inc(done, 1)
                dve.wait_ge(done, at + SOME)
                dve.tensor_tensor(small[:, :], few[:, :], some[:, :], ALU.mult).then_inc(done, 1)
                dve.wait_ge(done, at + CODE)
                if with_hits:
                    dve.tensor_tensor(hit[:, :, :], diag_codes[:, i % 2, :, :],
                                      code[:, :].unsqueeze(1).broadcast_to([P, P, NB]),
                                      ALU.is_equal).then_inc(done, 1)
                else:
                    dve.tensor_tensor(changed[:, :], gap[:, 0, :], gap[:, 1, :], ALU.not_equal).then_inc(done, 1)
                dve.wait_ge(done, at + PARITY)
                dve.scalar_tensor_tensor(even[:, :], parity[:, :], 1.0 - SHIFT, few[:, :], ALU.is_gt,
                                         ALU.is_gt).then_inc(done, 1)

            def codes_of(i, done, at):
                up_code, up_from, low_bias, low_code, low_scale = (rule[:, k, i % 2, :] for k in range(5))
                dve.tensor_tensor(edge_a[:, :], even[:, :], last_at[:, :], ALU.mult).then_inc(done, 1)
                dve.tensor_tensor(left[:, :], left_low[:, :], removed, ALU.subtract).then_inc(done, 1)
                dve.tensor_tensor(mid_a[:, :], last_code[:, :], code[:, :], ALU.subtract).then_inc(done, 1)
                dve.wait_ge(done, at + 1)
                dve.scalar_tensor_tensor(edge_b[:, :], small[:, :], FAR - ALL, edge_a[:, :], ALU.mult,
                                         ALU.add).then_inc(done, 1)
                dve.wait_ge(done, at + 3)
                dve.scalar_tensor_tensor(mid_b[:, :], mid_a[:, :], 0.5, even[:, :], ALU.mult,
                                         ALU.mult).then_inc(done, 1)
                dve.tensor_tensor(mid_c[:, :], left[:, :], code[:, :], ALU.add).then_inc(done, 1)
                dve.wait_ge(done, at + 4)
                dve.tensor_scalar(up_from, edge_b[:, :], -1.0, FAR, ALU.mult, ALU.add).then_inc(done, 1)
                dve.wait_ge(done, at + 6)
                dve.tensor_tensor(low_code, mid_b[:, :], few[:, :], ALU.subtract).then_inc(done, 1)
                dve.tensor_scalar(low_scale, small[:, :], -1.0, 1.0, ALU.mult, ALU.add).then_inc(done, 1)
                dve.tensor_copy(up_code, code[:, :]).then_inc(done, 1)
                dve.wait_ge(done, at + 8)
                dve.scalar_tensor_tensor(low_bias, mid_c[:, :], -1.0, low_code, ALU.mult,
                                         ALU.subtract).then_inc(done, 1)

            def final(i):
                g = sweep_number(i, SWEEPS[i])
                dve.wait_ge(removed_ready, g + 1)
                dve.wait_ge(sweep_step, STEPS * g)
                sweep(i, gap[:, SWEEPS[i] % 2, :], sweep_step, STEPS * g, False)
                dve.wait_ge(sweep_step, STEPS * (g + 1))
                if i >= 2:
                    dve.wait_ge(ps_free["L"], (i - 1) * NB)
                codes_of(i, final_step, i * CODES)

            def test(i):
                dve.wait_ge(flag_ps, i + 1)
                dve.tensor_reduce(flag[:, :], spare[0:1, 0:NB], AX.X, ALU.max).then_inc(flag_ready, 1)
                dve.wait_ge(flag_ready, i + 1)
                more = dve.value_load(flag[0:1, 0:1], min_val=0, max_val=P)
                dve.wait_ge(final_step, (i + 1) * CODES)
                with dve.If(more > 0):
                    with dve.Fori(0, P) as k:
                        sweep(i, gap[:, 0, :], more_step[i], k * STEPS, True)
                        dve.wait_ge(more_step[i], k * STEPS + EVEN)
                        dve.wait_ge(more_removed[i], k + 1)
                    sweep(i, gap[:, 0, :], more_step[i], P * STEPS, False)
                    dve.wait_ge(more_step[i], (P + 1) * STEPS)
                    codes_of(i, more_step[i], (P + 1) * STEPS)
                    dve.wait_ge(more_step[i], (P + 1) * STEPS + CODES)

            def mark_up(i, b):
                n = i * NB + b
                width = N - i * P
                if n >= 2:
                    dve.wait_ge(ps_ready["P"], n - 1)
                for k, op in ((0, ALU.is_equal), (1, ALU.is_ge)):
                    dve.tensor_scalar(hits("U", b)[k][:, 0:width], ranks[:, i % 2, b, 0:width],
                                      rule[:, k, i % 2, b:b + 1], None, op).then_inc(hits_up, 1)

            def mark_low(i, b):
                n = i * NB + b
                width = (i + 1) * P
                dve.wait_ge(ps_free["V"], n + 1)
                if n >= 2:
                    dve.wait_ge(ps_ready["L"], n - 1)
                dve.tensor_scalar(hits("L", b)[0][:, 0:width], low_codes[:, b % 2, 0:width],
                                  rule[:, 3, i % 2, b:b + 1], None, ALU.is_equal).then_inc(hits_low, 1)

            def norm_input(b):
                xb = rT[:, b, :].rearrange("p (t d) -> p t d", t=NT)
                dve.wait_ge(x_in[b], 16)
                for t in range(NT):
                    dve.bn_stats(ln_stats[:, t, :], xb[:, t, :]).then_inc(ln_stat, 1)
                n = 2 * NT * b
                for t in range(NT):
                    dve.wait_ge(ln_stat, n + NT)
                    dve.bn_aggr(ln_mv[:, b % 2, t, :], ln_stats[:, t, :]).then_inc(ln_stat, 1)
                dve.wait_ge(ln_stat, n + 2 * NT)
                dve.tensor_scalar(ln_std[:, 0, :], ln_mv[:, b % 2, :, 1], LN_EPS, None, ALU.add).then_inc(ln_var, 1)
                inv, less = ln_inv[:, 0, b % 2, :], ln_inv[:, 1, b % 2, :]
                if b >= 2:
                    dve.wait_ge(ln_done, (b - 1) * ACT_TILES)
                dve.wait_ge(ln_root, b + 1)
                dve.reciprocal(inv, ln_std[:, 1, :]).then_inc(ln_scale, 1)
                dve.wait_ge(ln_scale, 2 * b + 1)
                dve.scalar_tensor_tensor(less, ln_mv[:, b % 2, :, 0], -1.0, inv, ALU.mult, ALU.mult
                                         ).then_inc(ln_scale, 1)
                for t in range(ACT_TILES, NT):
                    dve.tensor_scalar(xb[:, t, :], xb[:, t, :], ln_mv[:, b % 2, t, 0:1], inv[:, t:t + 1],
                                      ALU.subtract, ALU.mult).then_inc(ln_done_dve, 1)

            def bound_inputs():
                dve.wait_ge(weights_in, 16 * (4 * LAYERS + 1))
                dve.memset(reach[:, 0, 0:1], float(D) ** 0.5).then_inc(reach_step, 1)
                gains = columns[:, NB * NT:NB * NT + LAYERS - 1]
                shifts = columns[:, NB * NT + LAYERS:NB * NT + 2 * LAYERS - 1]
                dve.tensor_scalar(reach[:, 1, 0:2], gains, -1.0, None, ALU.mult).then_inc(reach_step, 1)
                dve.tensor_scalar(reach[:, 2, 0:2], shifts, -1.0, None, ALU.mult).then_inc(reach_step, 1)
                dve.wait_ge(reach_step, 3)
                dve.tensor_tensor(reach[:, 1, 0:2], reach[:, 1, 0:2], gains, ALU.max).then_inc(reach_step, 1)
                dve.tensor_tensor(reach[:, 2, 0:2], reach[:, 2, 0:2], shifts, ALU.max).then_inc(reach_step, 1)
                dve.wait_ge(reach_step, 5)
                dve.scalar_tensor_tensor(reach[:, 0, 1:3], reach[:, 1, 0:2], float(NB * N) ** 0.5 * 1.01,
                                         reach[:, 2, 0:2], ALU.mult, ALU.add).then_inc(reach_step, 1)
                dve.wait_ge(reach_step, 6)

            def bound_operands(l):
                if l:
                    dve.wait_ge(reach_ps, l)
                dve.tensor_scalar(wabs[:, :], wraw[:, l, 0:D], -1.0, None, ALU.mult).then_inc(reach_made, 1)
                dve.tensor_copy(reach_wide[:, :], reach[:, 0, l:l + 1].broadcast_to([P, P])).then_inc(reach_made, 1)
                dve.wait_ge(reach_made, 3 * l + 2)
                dve.tensor_tensor(wabs[:, :], wabs[:, :], wraw[:, l, 0:D], ALU.max).then_inc(reach_made, 1)

            def bound(l):
                dve.wait_ge(reach_ps, l + 1)
                n = 6 + 5 * l
                up, back = zscale[:, 0, l:l + 1], zscale[:, 1, l:l + 1]
                dve.tensor_reduce(back, spare[:, D:2 * D], AX.X, ALU.max).then_inc(reach_step, 1)
                dve.wait_ge(reach_step, n + 1)
                dve.tensor_scalar(back, back, 1e-30, None, ALU.max).then_inc(reach_step, 1)
                dve.wait_ge(reach_step, n + 2)
                dve.tensor_scalar(back.bitcast(I32), back.bitcast(I32), 0x7F800000, None,
                                  ALU.bitwise_and).then_inc(reach_step, 1)
                dve.wait_ge(reach_step, n + 3)
                dve.tensor_scalar(back, back, 1.0 / TOP, None, ALU.mult).then_inc(reach_step, 1)
                dve.wait_ge(reach_step, n + 4)
                dve.reciprocal(up, back).then_inc(reach_step, 1)
                dve.wait_ge(reach_step, n + 5)

            for kind, i, b in TASKS:
                if kind == "Z":
                    if i == 0:
                        mask_columns()
                    setup(i)
                elif kind == "S":
                    level(i)
                elif kind == "W":
                    g = sweep_number(i, b)
                    dve.wait_ge(removed_ready, g + 1)
                    if g:
                        dve.wait_ge(sweep_step, STEPS * g)
                    sweep(i, gap[:, b % 2, :], sweep_step, STEPS * g, True)
                elif kind == "F":
                    final(i)
                elif kind == "T":
                    test(i)
                elif kind == "P":
                    mark_up(i, b)
                elif kind == "K":
                    mark_low(i, b)
                elif kind == "Q":
                    if i == 0:
                        bound_inputs()
                    bound_operands(i)
                elif kind == "B":
                    bound(i)
                elif kind == "N":
                    norm_input(b)

            for k in "CPVLMH":
                dve.wait_ge(ps_free[k], NB if k == "H" else NT * NB)
            dve.memset(affine[:, 0:1], 1.0).then_inc(prep_step, 1)
            dve.memset(affine[:, 1:2], 0.0).then_inc(prep_step, 1)
            dve.wait_ge(prep_step, 2)

            def products(l, b, steps=range(NT // 2), beside_head=False):
                for k in steps:
                    n = (l * NB + b) * 4 + k
                    dve.wait_ge(prod_ready, n + 1)
                    dve.tensor_tensor(zo[:, b % 2, 2 * k:2 * k + 2, :],
                                      product_bank(k, beside_head)[:, :].rearrange("p (t c) -> p t c", t=2),
                                      rowconst[:, :].unsqueeze(1).broadcast_to([P, 2, 2 * D]),
                                      ALU.add).then_inc(prod_free, 1)

            def combine(l, b, steps):
                for k in steps:
                    n = (l * NB + b) * 4 + k
                    dve.wait_ge(agg_ready, n + 1)
                    ps = agg_ps[:, k % 2, :, :]
                    dve.tensor_scalar(degree[:, 0, :], ps[:, :, 2 * D], 1.0, None, ALU.max).then_inc(sage_step, 1)
                    dve.tensor_reduce(part_sum[:, k % 2, :, :], ps[:, :, 0:2 * D].rearrange(
                        "p t (s d) -> p t d s", s=2), AX.X, ALU.add).then_inc(sage_step, 1)
                    dve.wait_ge(sage_step, 4 * n + 1)
                    dve.reciprocal(degree[:, 1, :], degree[:, 0, :]).then_inc(sage_step, 1)
                    dve.wait_ge(sage_step, 4 * n + 3)
                    dve.tensor_scalar(degree[:, 1, :], degree[:, 1, :], zback[:, :], None, ALU.mult
                                      ).then_inc(sage_step, 1)
                    dve.wait_ge(sage_step, 4 * n + 4)
                    for h in range(2):
                        t = 2 * k + h
                        dve.scalar_tensor_tensor(sage[:, b % 2, t, :], part_sum[:, k % 2, h, :],
                                                 degree[:, 1, h:h + 1], zo[:, b % 2, t, D:2 * D],
                                                 ALU.mult, ALU.add).then_inc(sage_ready, 1)
                    dve.wait_ge(sage_ready, 2 * (n + 1))

            def unit(l, b):
                n = l * NB + b
                dve.wait_ge(root_ready, n + 1)
                dve.tensor_scalar(norms[:, 2, :], norms[:, 1, :], NORM_EPS, None, ALU.max).then_inc(norm_step, 1)
                dve.wait_ge(norm_step, 3 * n + 1)
                dve.reciprocal(norms[:, 3, :], norms[:, 2, :]).then_inc(norm_step, 1)
                dve.wait_ge(norm_step, 3 * n + 2)
                dve.tensor_tensor(norms[:, 3, :], norms[:, 3, :], mask[:, b, :], ALU.mult).then_inc(norm_step, 1)
                dve.wait_ge(norm_step, 3 * n + 3)
                dve.tensor_tensor(sage[:, b % 2, :, :], sage[:, b % 2, :, :],
                                  norms[:, 3, :].unsqueeze(2).broadcast_to([P, NT, D]),
                                  ALU.mult).then_inc(unit_ready, 1)
                dve.wait_ge(unit_ready, n + 1)

            def batch_norm(l):
                c = l * BN
                dve.wait_ge(moments_ready, 2 * NB * (l + 1))
                dve.tensor_reduce(bn[:, 0:2], moments[:, :, :], AX.X, ALU.add).then_inc(bn_step, 1)
                dve.wait_ge(bn_step, c + 1)
                dve.tensor_scalar(bn[:, 2:4], bn[:, 0:2], 1.0 / (NB * N), None, ALU.mult).then_inc(bn_step, 1)
                dve.wait_ge(bn_step, c + 2)
                dve.tensor_tensor(bn[:, 4:5], bn[:, 2:3], bn[:, 2:3], ALU.mult).then_inc(bn_step, 1)
                dve.wait_ge(bn_step, c + 3)
                dve.tensor_tensor(bn[:, 5:6], bn[:, 3:4], bn[:, 4:5], ALU.subtract).then_inc(bn_step, 1)
                dve.wait_ge(bn_step, c + 4)
                dve.tensor_scalar(bn[:, 6:7], bn[:, 5:6], 0.0, BN_EPS, ALU.max, ALU.add).then_inc(bn_var, 1)
                dve.wait_ge(bn_root, l + 1)
                dve.reciprocal(bn[:, 8:9], bn[:, 7:8]).then_inc(bn_step, 1)
                dve.wait_ge(bn_step, c + 5)
                gcol = columns[:, bass.ds(l + NB * NT, 1)]
                bcol = columns[:, bass.ds(l + NB * NT + LAYERS, 1)]
                dve.tensor_tensor(affine[:, 0:1], gcol, bn[:, 8:9], ALU.mult).then_inc(bn_step, 1)
                dve.wait_ge(bn_step, c + 6)
                dve.tensor_tensor(bn[:, 4:5], bn[:, 2:3], affine[:, 0:1], ALU.mult).then_inc(bn_step, 1)
                dve.wait_ge(bn_step, c + 7)
                dve.tensor_tensor(affine[:, 1:2], bcol, bn[:, 4:5], ALU.subtract).then_inc(bn_step, 1)
                dve.wait_ge(bn_step, c + 8)

            def head_weights(l):
                lw = wraw[:, bass.ds(l, 1), :].rearrange("p a c -> p (a c)")
                dve.tensor_copy(wcur[:, 2 * D:3 * D], lw[:, 2 * D:3 * D]).then_inc(head_step, 1)
                dve.wait_ge(head_step, 2 * l + 1)

            def head_constant(l):
                dve.tensor_tensor(head_const[:, :], head_const[:, :], prod_ps[0][:, 2 * D:3 * D], ALU.add
                                  ).then_inc(head_step, 1)

            def head_rows(l, b, halves=(0, 1), beside_products=False):
                for h in halves:
                    dve.wait_ge(y_ps, (l * NB + b) * 2 + h + 1)
                    dve.tensor_tensor(ysum[:, b, 4 * h:4 * h + 4, :], ysum[:, b, 4 * h:4 * h + 4, :],
                                      head_bank(h, beside_products)[:, :].rearrange("p (t d) -> p t d", t=4),
                                      ALU.add).then_inc(y_added, 1)

            def layer(l, first):
                at = 2 + l * PREP
                lw = wraw[:, bass.ds(l, 1), :].rearrange("p a c -> p (a c)")
                dve.tensor_scalar(wcur[:, 0:D], lw[:, 0:D], zscale[:, 0, bass.ds(l, 1)], None, ALU.mult
                                  ).then_inc(prep_step, 1)
                dve.tensor_copy(zback[:, :], zscale[:, 1, bass.ds(l, 1)]).then_inc(prep_step, 1)
                dve.tensor_copy(wcur[:, D:2 * D], lw[:, D:2 * D]).then_inc(prep_step, 1)
                if not first:
                    head_weights(l - 1)
                    batch_norm(l - 1)
                width = 2 * D if first else 3 * D
                dve.tensor_copy(shift_wide[:, :], affine[:, 1:2].broadcast_to([P, P])).then_inc(wide_ready, 1)
                dve.wait_ge(prep_step, at + 3)
                dve.tensor_scalar(wscaled[:, 0:width], wcur[:, 0:width], affine[:, 0:1], None, ALU.mult
                                  ).then_inc(wide_ready, 1)
                dve.wait_ge(rowconst_ps, l + 1)
                bw = bias_wide[:, bass.ds(l, 1), :].rearrange("p a c -> p (a c)")
                dve.tensor_tensor(rowconst[:, :], prod_ps[0][:, 0:2 * D], bw, ALU.add).then_inc(prep_step, 1)
                if not first:
                    head_constant(l - 1)
                dve.wait_ge(prep_step, at + PREP)
                products(l, 0)
                products(l, 1)
                for b in range(NB):
                    for k in range(4):
                        combine(l, b, [k])
                        if k == 0 and b and first:
                            unit(l, b - 1)
                        if b + 2 < NB:
                            products(l, b + 2, [k], b and not first)
                        if k < 2 and b and not first:
                            head_rows(l - 1, b - 1, [k], b + 2 < NB)
                        if k == 0 and b and not first:
                            unit(l, b - 1)
                unit(l, NB - 1)
                if not first:
                    head_rows(l - 1, NB - 1)
                    dve.wait_ge(y_added, l * 2 * NB)

            PREP, BN = 4, 8
            layer(0, True)
            dve.wait_ge(ysum_cleared, 1)
            with dve.Fori(1, LAYERS) as l:
                layer(l, False)
            l = LAYERS - 1
            head_weights(l)
            batch_norm(l)
            dve.tensor_copy(shift_wide[:, :], affine[:, 1:2].broadcast_to([P, P])).then_inc(wide_ready, 1)
            dve.tensor_scalar(wscaled[:, 2 * D:3 * D], wcur[:, 2 * D:3 * D], affine[:, 0:1], None, ALU.mult
                              ).then_inc(wide_ready, 1)
            dve.wait_ge(rowconst_ps, LAYERS + 1)
            dve.wait_ge(head_step, 2 * l + 1)
            head_constant(l)
            dve.wait_ge(head_step, 2 * LAYERS)
            for b in range(NB):
                head_rows(l, b)
                dve.wait_ge(y_added, (l * NB + b + 1) * 2)
                dve.tensor_tensor(ysum[:, b, :, :], ysum[:, b, :, :],
                                  head_const[:, :].unsqueeze(1).broadcast_to([P, NT, D]), ALU.add
                                  ).then_inc(last_step, 1)

        @block.scalar
        def _(act):
            for kind, i, b in TASKS:
                if kind == "C":
                    use = ("C", i, b)
                    act.wait_ge(ps_ready["C"], count(use))
                    if i >= 2:
                        act.wait_ge(hits_up, 2 * ((i - 2) * NB + b + 1))
                    act.activation(ranks[:, i % 2, b, 0:N - i * P], slot(use)[:, 0:N - i * P], ACT.Copy,
                                   bias=-SHIFT).then_inc(ps_free["C"], 1)
                elif kind == "P":
                    use = ("P", i, b)
                    act.wait_ge(ps_ready["P"], count(use))
                    act.activation(graph[:, i, b, i * P:N], slot(use)[:, 0:N - i * P], ACT.Copy,
                                   saturate=False).then_inc(ps_free["P"], 1)
                elif kind == "V":
                    use = ("V", i, b)
                    act.wait_ge(ps_ready["V"], count(use))
                    n = count(use)
                    if n > 2:
                        act.wait_ge(hits_low, n - 2)
                    act.activation(low_codes[:, b % 2, 0:(i + 1) * P], slot(use)[:, 0:(i + 1) * P], ACT.Abs,
                                   bias=rule[:, 2, i % 2, b:b + 1]).then_inc(ps_free["V"], 1)
                elif kind == "L":
                    use = ("L", i, b)
                    act.wait_ge(ps_ready["L"], count(use))
                    act.activation(graph[:, i, b, 0:(i + 1) * P], slot(use)[:, 0:(i + 1) * P], ACT.Copy,
                                   scale=rule[:, 4, i % 2, b:b + 1], saturate=False).then_inc(ps_free["L"], 1)
                elif kind == "M":
                    act.wait_ge(ps_ready["M"], count(("M", i, b)))
                    act.activation(graph[:, 0:i + 1, b, i * P:(i + 1) * P],
                                   slot(("M", i, b))[:, 0:(i + 1) * P].rearrange("p (j c) -> p j c", j=i + 1),
                                   ACT.Sign, saturate=False).then_inc(ps_free["M"], 1)
                elif kind == "N":
                    act.wait_ge(ln_var, b + 1)
                    act.activation(ln_std[:, 1, :], ln_std[:, 0, :], ACT.Sqrt).then_inc(ln_root, 1)
                    act.wait_ge(ln_scale, 2 * (b + 1))
                    xb = rT[:, b, :].rearrange("p (t d) -> p t d", t=NT)
                    for t in range(ACT_TILES):
                        act.activation(xb[:, t, :], xb[:, t, :], ACT.Identity,
                                       scale=ln_inv[:, 0, b % 2, t:t + 1],
                                       bias=ln_inv[:, 1, b % 2, t:t + 1]).then_inc(ln_done, 1)
                elif kind == "H":
                    act.wait_ge(ps_ready["H"], b + 1)
                    act.activation(rT[:, b, :], slot(("H", 0, b)), ACT.Relu).then_inc(ps_free["H"], 1)

            def top(l, b):
                act.wait_ge(prod_free, (l * NB + b + 1) * 4)
                act.activation(parts[:, b % 2, :, 0:D], zo[:, b % 2, :, 0:D], ACT.Copy).then_inc(top_ready, 1)

            def lengths(l, b, tiles):
                n = l * NB + b
                if b and tiles[0] == 0:
                    act.wait_ge(root_ready, n)
                for t in tiles:
                    if t % 2 == 0:
                        act.wait_ge(sage_ready, n * NT + t + 2)
                    act.activation(squares[:, t * D:(t + 1) * D], sage[:, b % 2, t, :], ACT.Square,
                                   accum_out=norms[:, 0, t:t + 1]).then_inc(squared, 1)
                if t < NT - 1:
                    return
                act.wait_ge(squared, (n + 1) * NT)
                act.activation(norms[:, 1, :], norms[:, 0, :], ACT.Sqrt).then_inc(root_ready, 1)

            def turn_out(l, b):
                n = l * NB + b
                act.wait_ge(turn_ready, n + 1)
                act.activation(rT[:, b, :], turn_ps, ACT.Relu, accum_out=moments[:, 0, b:b + 1]
                               ).then_inc(moments_ready, 1)
                act.wait_ge(moments_ready, 2 * n + 1)
                act.activation(squares, rT[:, b, :], ACT.Square, accum_out=moments[:, 1, b:b + 1]
                               ).then_inc(moments_ready, 1)
                act.wait_ge(moments_ready, 2 * n + 2)

            act.wait_ge(pool_step, 10 + 1 + 1)
            with act.Fori(0, LAYERS) as l:
                top(l, 0)
                top(l, 1)
                for b in range(NB):
                    lengths(l, b, range(NT // 2))
                    if b:
                        turn_out(l, b - 1)
                    lengths(l, b, range(NT // 2, NT))
                    if b + 2 < NB:
                        top(l, b + 2)
                turn_out(l, NB - 1)
                act.wait_ge(bn_var, l + 1)
                act.activation(bn[:, 7:8], bn[:, 6:7], ACT.Sqrt).then_inc(bn_root, 1)
            for b in range(NB):
                act.wait_ge(last_step, b + 1)
                for t in range(NT):
                    act.activation(ysum[:, b, t, :], ysum[:, b, t, :], ACT.Copy,
                                   scale=columns[:, b * NT + t:b * NT + t + 1]).then_inc(scaled, 1)

        @block.tensor
        def _(pe):
            def mm(out_, lhsT, rhs, start, stop):
                return pe.matmul(out_, lhsT, rhs, start=start, stop=stop)

            pe.wait_ge(consts_made, 7)
            pe.wait_ge(rows_ready, 1)
            pe.wait_ge(params_in, 16 * 2 * LAYERS)
            nv = NB * NT + 2 * LAYERS
            mm(spare[:, 0:nv], vectors[:, :], eye32[0:nv, 0:nv], True, True).then_inc(columns_ps, 1)

            def ready_slot(use):
                for old in BEFORE[use]:
                    pe.wait_ge(ps_free[old[0]], count(old))

            def original(i, j, b):
                return diag_low[:, i % 2, b, :] if i == j else graph[:, j, b, i * P:(i + 1) * P]

            def prefix(ps, tiles, width):
                for first, (at, tile) in enumerate(tiles):
                    for lo, hi in pieces(at, width):
                        last = mm(ps[:, lo:hi], tile, stair[:, lo - at:hi - at], first == 0,
                                  at + P >= min(width, (lo // BANK + 1) * BANK))
                return last

            def minus(ps, marks, width):
                for row in marks:
                    for lo, hi in pieces(0, width):
                        last = mm(ps[:, lo:hi], neg_eye[:, :], row[:, lo:hi], False, row is marks[-1])
                return last

            def upper_ranks(i, b):
                use = ("C", i, b)
                ready_slot(use)
                pe.wait_ge(triangles_ready, 2 * (i + 1))
                prefix(slot(use), [((j - i) * P, original(i, j, b)) for j in range(i, NT)],
                       N - i * P).then_inc(ps_ready["C"], 1)

            def right_counts(i):
                pe.wait_ge(triangles_ready, 2 * (i + 1))
                if i == 0:
                    pe.wait_ge(columns_ready, 1)
                for b in range(NB):
                    for j in range(i, NT):
                        last = mm(right_ps[:, b:b + 1], original(i, j, b), ones[:, :], b == 0 and j == i,
                                  j == NT - 1 and b == NB - 1)
                last.then_inc(right_ready, 1)

            def left_counts(i):
                if i:
                    pe.wait_ge(final_step, i * CODES)
                mm(removed, eye[:, :], zeros[:, :], True, False)
                for b in range(NB):
                    if i:
                        pe.wait_ge(ps_free["P"], (i - 1) * NB + b + 1)
                    for j in range(i):
                        mm(left_ps[:, b:b + 1], graph[:, j, b, i * P:(i + 1) * P], ones[:, :], False, False)
                    last = mm(left_ps[:, b:b + 1], diag_up[:, i % 2, b, :], ones[:, :], False, b == NB - 1)
                last.then_inc(removed_ready, 1)

            def count_removed(i, done, at):
                pe.wait_ge(done, at)
                for b in range(NB):
                    mm(removed[:, b:b + 1], diag_up[:, i % 2, b, :], small[:, b:b + 1], b == 0, False)
                for b in range(NB):
                    mm(removed[:, b:b + 1], last_edge[:, :, b], even[:, b:b + 1], False, False)
                for b in range(NB):
                    last = mm(removed[:, b:b + 1], hit[:, :, b], ones[:, :], False, b == NB - 1)
                return last

            def count_changes(i):
                g = sweep_number(i, SWEEPS[i])
                pe.wait_ge(sweep_step, STEPS * g + HIT)
                if i:
                    pe.wait_ge(flag_ready, i)
                pe.matmul(spare[0:1, 0:NB], ones[:, :], changed[:, :], start=True, stop=True).then_inc(flag_ps, 1)

            def test(i):
                pe.wait_ge(flag_ready, i + 1)
                more = pe.value_load(flag[0:1, 0:1], min_val=0, max_val=P)
                with pe.If(more > 0):
                    with pe.Fori(0, P) as k:
                        count_removed(i, more_step[i], (k + 1) * STEPS).then_inc(more_removed[i], 1)

            def rows_after(i, b):
                use = ("P", i, b)
                ready_slot(use)
                ps, width = slot(use), N - i * P
                for j in range(i, NT):
                    at = (j - i) * P
                    mm(ps[:, at:at + P], original(i, j, b), eye[:, :], at % BANK == 0, False)
                pe.wait_ge(hits_up, 2 * (i * NB + b + 1))
                minus(ps, hits("U", b), width).then_inc(ps_ready["P"], 1)

            def lower_ranks(i, b):
                use = ("V", i, b)
                ready_slot(use)
                pe.wait_ge(ps_free["P"], i * NB + b + 1)
                prefix(slot(use), [(j * P, graph[:, j, b, i * P:(i + 1) * P]) for j in range(i + 1)],
                       (i + 1) * P).then_inc(ps_ready["V"], 1)

            def kept(i, b):
                use = ("L", i, b)
                ready_slot(use)
                ps, width = slot(use), (i + 1) * P
                for j in range(i + 1):
                    mm(ps[:, j * P:(j + 1) * P], graph[:, j, b, i * P:(i + 1) * P], eye[:, :],
                       j * P % BANK == 0, False)
                pe.wait_ge(hits_low, i * NB + b + 1)
                minus(ps, hits("L", b), width).then_inc(ps_ready["L"], 1)

            def mirror(i, b):
                use = ("M", i, b)
                ready_slot(use)
                pe.wait_ge(ps_free["L"], i * NB + b + 1)
                ps = slot(use)
                for j in range(i + 1):
                    mm(ps[:, j * P:(j + 1) * P], graph[:, i, b, j * P:(j + 1) * P], eye[:, :],
                       j * P % BANK == 0, j < i and (j + 1) * P % BANK == 0)
                mm(ps[:, i * P:(i + 1) * P], eye[:, :], graph[:, i, b, i * P:(i + 1) * P], False, True
                   ).then_inc(ps_ready["M"], 1)

            for kind, i, b in TASKS:
                if kind == "C":
                    upper_ranks(i, b)
                elif kind == "U":
                    right_counts(i)
                elif kind == "S":
                    left_counts(i)
                elif kind == "W":
                    g = sweep_number(i, b)
                    count_removed(i, sweep_step, STEPS * (g + 1)).then_inc(removed_ready, 1)
                elif kind == "F":
                    count_changes(i)
                elif kind == "T":
                    test(i)
                elif kind == "P":
                    rows_after(i, b)
                elif kind == "V":
                    lower_ranks(i, b)
                elif kind == "L":
                    kept(i, b)
                elif kind == "M":
                    mirror(i, b)
                elif kind == "R":
                    pe.wait_ge(reach_made, 3 * (i + 1))
                    if i:
                        pe.wait_ge(reach_step, 6 + 5 * i)
                    mm(spare[:, D:2 * D], reach_wide[:, :], wabs[:, :], True, True).then_inc(reach_ps, 1)
                elif kind == "H":
                    use = ("H", 0, b)
                    ready_slot(use)
                    pe.wait_ge(ln_done, (b + 1) * ACT_TILES)
                    pe.wait_ge(ln_done_dve, (b + 1) * (NT - ACT_TILES))
                    for t in range(NT):
                        last = pe.transpose(slot(use)[:, t * P:(t + 1) * P], rT[:, b, t * P:(t + 1) * P],
                                            eye32[:, :])
                    last.then_inc(ps_ready["H"], 1)

            for k in "CPVLMH":
                pe.wait_ge(ps_free[k], NB if k == "H" else NT * NB)

            def products(l, b, steps, beside_head):
                for k in steps:
                    n = (l * NB + b) * 4 + k
                    if beside_head and k == 3:
                        pe.wait_ge(y_added, ((l - 1) * NB + b - 3 + 1) * 2)
                    elif beside_head and k:
                        pe.wait_ge(prod_free, n)
                    elif b or k >= 2:
                        pe.wait_ge(prod_free, n - 1)
                    for t in (2 * k, 2 * k + 1):
                        last = mm(product_bank(k, beside_head)[:, (t % 2) * 2 * D:(t % 2 + 1) * 2 * D],
                                  rT[:, b, t * P:(t + 1) * P], wscaled[:, 0:2 * D], True, True)
                    last.then_inc(prod_ready, 1)

            def aggregate(l, b, k):
                n = (l * NB + b) * 4 + k
                if k == 0:
                    pe.wait_ge(low_ready, l * NB + b + 1)
                if b or k >= 2:
                    pe.wait_ge(sage_ready, 2 * (n - 1))
                mm(agg_ps[:, k % 2, 0, 0:1], eye[:, :], ones[:, :], True, True)
                for h in range(2):
                    t = 2 * k + h
                    for j in range(NT):
                        last = mm(agg_ps[:, k % 2, h, 0:WZ], graph[:, j, b, t * P:(t + 1) * P],
                                  parts[:, b % 2, j, 0:WZ], j == 0, j == NT - 1)
                last.then_inc(agg_ready, 1)

            def turn(l, b):
                n = l * NB + b
                pe.wait_ge(unit_ready, n + 1)
                if b:
                    pe.wait_ge(moments_ready, 2 * n)
                for t in range(NT):
                    last = pe.transpose(turn_ps[:, t * P:(t + 1) * P], sage[:, b % 2, t, :], eye32[:, :])
                last.then_inc(turn_ready, 1)

            def head_rows(l, b, h, beside_products, after_products):
                if after_products:
                    pe.wait_ge(prod_free, ((l + 1) * NB + b + 3) * 4)
                elif beside_products:
                    pe.wait_ge(y_added, (l * NB + b) * 2 + 1)
                elif b:
                    pe.wait_ge(y_added, (l * NB + b - 1) * 2 + h + 1)
                for t in range(4):
                    last = mm(head_bank(h, beside_products)[:, t * D:(t + 1) * D],
                              rT[:, b, (4 * h + t) * P:(4 * h + t + 1) * P],
                              wscaled[:, 2 * D:3 * D], True, True)
                last.then_inc(y_ps, 1)

            def layer(l, first):
                pe.wait_ge(wide_ready, 2 * (l + 1))
                width = 2 * D if first else 3 * D
                mm(prod_ps[0][:, 0:width], shift_wide[:, :], wcur[:, 0:width], True, True
                   ).then_inc(rowconst_ps, 1)
                if not first:
                    pe.wait_ge(head_step, 2 * l)
                pe.wait_ge(prep_step, 2 + 4 * (l + 1))
                products(l, 0, range(4), False)
                products(l, 1, range(4), False)
                for b in range(NB):
                    more = b + 2 < NB
                    for k in range(4):
                        aggregate(l, b, k)
                        if more:
                            products(l, b + 2, [k], b and not first)
                        if k < 2 and b and not first:
                            head_rows(l - 1, b - 1, k, more, k == 0 if more else b + 2 == NB)
                        if k == 1 and b:
                            turn(l, b - 1)
                if not first:
                    for h in range(2):
                        head_rows(l - 1, NB - 1, h, False, False)
                turn(l, NB - 1)

            layer(0, True)
            with pe.Fori(1, LAYERS) as l:
                layer(l, False)
            l = LAYERS - 1
            pe.wait_ge(wide_ready, 2 * (LAYERS + 1))
            mm(prod_ps[0][:, 2 * D:3 * D], shift_wide[:, :], wcur[:, 2 * D:3 * D], True, True
               ).then_inc(rowconst_ps, 1)
            pe.wait_ge(head_step, 2 * LAYERS)
            for b in range(NB):
                for h in range(2):
                    head_rows(l, b, h, False, False)


_OUT = (NB, N, D)


def kernel(**inputs):
    import numpy as np
    import concourse.bacc as bacc
    from concourse.bass_utils import run_bass_kernel_spmd as run

    nc = bacc.Bacc("TRN2", target_bir_lowering=False, num_devices=1)
    arrays, aps = {}, {}
    for name, value in inputs.items():
        a = np.ascontiguousarray(value)
        arrays[f"in_{name}"] = a
        aps[name] = nc.dram_tensor(f"in_{name}", a.shape, mybir.dt.from_np(a.dtype), kind="ExternalInput").ap()
    result = nc.dram_tensor("result", _OUT, F32, kind="ExternalOutput").ap()

    def each(stem):
        return [aps[f"L0_gnn_{stem}{l}"] for l in (1, 2, 3)]

    build(nc, aps["x"], aps["adj"], aps["nodemask"], each("Wr"), each("Wx"), each("b"), each("g"),
          each("be"), aps["L0_gnn_Wl"], aps["L0_gnn_bl"], result)
    return run(nc, [arrays], core_ids=[0]).results[0]["result"]
```
